# Optimizing a Trainium2 kernel written in Bass

```python
import numpy as np
import jax
import jax.numpy as jnp

def _softmax(x, axis=-1):
    return jax.nn.softmax(x, axis=axis)

def _gelu(x):
    return jax.nn.gelu(x, approximate=True)

def _silu(x):
    return jax.nn.silu(x)

def _sigmoid(x):
    return jax.nn.sigmoid(x)

def _layernorm(x, axis=-1, eps=1e-05):
    m = jnp.mean(x, axis=axis, keepdims=True)
    v = jnp.var(x, axis=axis, keepdims=True)
    return (x - m) / jnp.sqrt(v + eps)

def _scatter_add(tgt, idx, src, axis=0):
    return tgt.at[idx].add(src)

def _segment_sum(src, seg, n):
    return jax.ops.segment_sum(src, seg, n)
kernel_name = 'mk_gnn_preln_d2_gnn_r64_2385e5'

def setup_inputs(seed: int=0):
    np.random.seed(seed)
    _w = jnp.asarray

    def _rec_inputs():
        import jax
        import jax.numpy as jnp
        _gk = jax.random.key(seed)
        x = -0.0001006 + 1 * jax.random.normal(jax.random.fold_in(_gk, 1), (50000, 96), jnp.float32)
        src = jax.random.randint(jax.random.fold_in(_gk, 2), (12500,), 0, 50000, jnp.int32)
        dst = jax.random.randint(jax.random.fold_in(_gk, 3), (12500,), 0, 50000, jnp.int32)
        _o = jnp.argsort(dst, stable=True)
        src = src[_o]
        dst = dst[_o]
        edge_attr_96 = 5.93493e-05 + 1.00006 * jax.random.normal(jax.random.fold_in(_gk, 12), (12500, 96), jnp.float32)
        return (x, src, dst, edge_attr_96)
    x, src, dst, edge_attr_96 = _rec_inputs()

    def _L0_gnn_setup():
        import jax, jax.numpy as jnp
        import numpy as np
        N_NODES = 50000
        N_EDGES = 12500
        H_FEATS = 96
        N_LAYERS = 3

        def _sage_conv(x, src, dst, W_self, W_neigh, b):
            msg = x[src]
            s = jax.ops.segment_sum(msg, dst, num_segments=N_NODES)
            deg = jax.ops.segment_sum(jnp.ones(src.shape, x.dtype), dst, num_segments=N_NODES)
            h_neigh = s / jnp.maximum(deg, 1.0)[:, None]
            return x @ W_self.T + b + h_neigh @ W_neigh.T
        key = jax.random.key(seed)
        k1, k2, k3, k4, k5 = jax.random.split(key, 5)
        in_feat = jax.random.normal(k1, (N_NODES, H_FEATS), dtype=jnp.float32)
        src = jax.random.randint(k2, (N_EDGES,), 0, N_NODES, dtype=jnp.int64)
        dst = jax.random.randint(k3, (N_EDGES,), 0, N_NODES, dtype=jnp.int64)
        scale = 1.0 / np.sqrt(H_FEATS)
        W_self = jax.random.uniform(k4, (H_FEATS, H_FEATS), jnp.float32, -scale, scale)
        W_neigh = jax.random.uniform(k5, (H_FEATS, H_FEATS), jnp.float32, -scale, scale)
        b = jnp.zeros((H_FEATS,), jnp.float32)
        return {'in_feat': in_feat, 'src': src, 'dst': dst, 'W_self': W_self, 'W_neigh': W_neigh, 'b': b}
    _L0_gnn_all = _L0_gnn_setup()
    _L0_gnn_in = {k: v for k, v in _L0_gnn_all.items() if k in ('W_self', 'W_neigh', 'b')}
    del _L0_gnn_all

    def _L1_gnn_setup():
        import jax, jax.numpy as jnp
        import numpy as np
        N_NODES = 50000
        N_EDGES = 12500
        NIN = 96
        NOUT = 96
        key = jax.random.key(seed)
        ks = jax.random.split(key, 10)
        s = 1.0 / np.sqrt(NIN)
        so = 1.0 / np.sqrt(NOUT)
        return {'x': jax.random.normal(ks[0], (N_NODES, NIN), dtype=jnp.float32), 'edge_index': jax.random.randint(ks[1], (2, N_EDGES), 0, N_NODES, dtype=jnp.int64), 'edge_attr': jax.random.normal(ks[2], (N_EDGES, NIN), dtype=jnp.float32), 'W_edge': jax.random.uniform(ks[3], (NIN, NIN), jnp.float32, -s, s), 'b_edge': jax.random.uniform(ks[4], (NIN,), jnp.float32, -s, s), 'eps': jnp.zeros((), dtype=jnp.float32), 'W1': jax.random.uniform(ks[5], (NOUT, NIN), jnp.float32, -s, s), 'b1': jax.random.uniform(ks[6], (NOUT,), jnp.float32, -s, s), 'W2': jax.random.uniform(ks[7], (NOUT, NOUT), jnp.float32, -so, so), 'b2': jax.random.uniform(ks[8], (NOUT,), jnp.float32, -so, so)}
    _L1_gnn_all = _L1_gnn_setup()
    _L1_gnn_in = {k: v for k, v in _L1_gnn_all.items() if k in ('W_edge', 'b_edge', 'eps', 'W1', 'b1', 'W2', 'b2')}
    del _L1_gnn_all
    return {'x': x, 'src': src, 'dst': dst, 'edge_attr_96': edge_attr_96, 'L0_gnn_W_self': _L0_gnn_in['W_self'], 'L0_gnn_W_neigh': _L0_gnn_in['W_neigh'], 'L0_gnn_b': _L0_gnn_in['b'], 'L1_gnn_W_edge': _L1_gnn_in['W_edge'], 'L1_gnn_b_edge': _L1_gnn_in['b_edge'], 'L1_gnn_eps': _L1_gnn_in['eps'], 'L1_gnn_W1': _L1_gnn_in['W1'], 'L1_gnn_b1': _L1_gnn_in['b1'], 'L1_gnn_W2': _L1_gnn_in['W2'], 'L1_gnn_b2': _L1_gnn_in['b2']}

def reference(x, src, dst, edge_attr_96, L0_gnn_W_self, L0_gnn_W_neigh, L0_gnn_b, L1_gnn_W_edge, L1_gnn_b_edge, L1_gnn_eps, L1_gnn_W1, L1_gnn_b1, L1_gnn_W2, L1_gnn_b2):
    import jax
    import jax.numpy as jnp

    def _L0_gnn_ref(in_feat, src, dst, W_self, W_neigh, b):
        import jax, jax.numpy as jnp
        import numpy as np
        N_NODES = 50000
        N_EDGES = 12500
        H_FEATS = 96
        N_LAYERS = 3

        def _sage_conv(x, src, dst, W_self, W_neigh, b):
            msg = x[src]
            s = jax.ops.segment_sum(msg, dst, num_segments=N_NODES)
            deg = jax.ops.segment_sum(jnp.ones(src.shape, x.dtype), dst, num_segments=N_NODES)
            h_neigh = s / jnp.maximum(deg, 1.0)[:, None]
            return x @ W_self.T + b + h_neigh @ W_neigh.T
        h = in_feat
        for i in range(N_LAYERS):
            h = _sage_conv(h, src, dst, W_self, W_neigh, b)
            if i < N_LAYERS - 1:
                h = jax.nn.relu(h)
        return h

    def _L1_gnn_ref(x, edge_index, edge_attr, W_edge, b_edge, eps, W1, b1, W2, b2):
        import jax, jax.numpy as jnp
        import numpy as np
        N_NODES = 50000
        N_EDGES = 12500
        NIN = 96
        NOUT = 96
        ea = edge_attr @ W_edge.T + b_edge
        src, dst = (edge_index[0], edge_index[1])
        msg = jax.nn.relu(x[src] + ea)
        aggr = jax.ops.segment_sum(msg, dst, num_segments=N_NODES)
        h = (1.0 + eps) * x + aggr
        h = jax.nn.relu(h @ W1.T + b1)
        return h @ W2.T + b2
    edge_index = jnp.stack([src, dst])
    h = jnp.maximum(_layernorm(x, axis=-1), 0.0)
    x = x + _L0_gnn_ref(h, src, dst, L0_gnn_W_self, L0_gnn_W_neigh, L0_gnn_b)
    h = jnp.maximum(_layernorm(x, axis=-1), 0.0)
    x = x + _L1_gnn_ref(h, edge_index, edge_attr_96, L1_gnn_W_edge, L1_gnn_b_edge, L1_gnn_eps, L1_gnn_W1, L1_gnn_b1, L1_gnn_W2, L1_gnn_b2)
    return x

_drawn_inputs = setup_inputs


def setup_inputs(seed=0):
    import zlib

    import numpy as np

    out = dict(_drawn_inputs(seed))
    spreads = {'L0_gnn_b': (0.0, 0.1)}
    factors = {'L1_gnn_b_edge': 8.0}
    for name, (base, spread) in spreads.items():
        noise = np.random.default_rng([zlib.crc32(name.encode()), seed]).standard_normal(out[name].shape)
        drawn = base * np.exp(spread * noise) if base else spread * noise
        out[name] = jnp.asarray(drawn.astype(out[name].dtype))
    for name, factor in factors.items():
        out[name] = (out[name] * factor).astype(out[name].dtype)
    return out
```

```python
from collections import Counter
from contextlib import ExitStack, contextmanager

import numpy as np

import concourse.bass as bass
from concourse import mybir

N_NODES = 50000
N_EDGES = 12500
H = 96
LN_EPS = 1e-5

P = 128
HALF = 5
UNIT = 2 * HALF
COLS = HALF * P
K1 = H + 1
PAIRS = -(-N_NODES // (UNIT * P))
ROWS = N_NODES // (P * UNIT) * UNIT
SLOTS = -(-N_EDGES // (UNIT * P)) * UNIT * P
ETILES = SLOTS // P
EUNITS = ETILES // UNIT
CHUNKS = 2 * EUNITS
FULL_ROWS = N_EDGES // P
REST = N_EDGES - FULL_ROWS * P
MAP_ROWS = 80
BIG = 1 << 17

f32, bf16, i32 = mybir.dt.float32, mybir.dt.bfloat16, mybir.dt.int32
ALU = mybir.AluOpType
ACT = mybir.ActivationFunctionType


class Tally:

    def __init__(self):
        self.base, self.now, self.per, self.i = Counter(), Counter(), {}, None

    def at(self, name, k=1):
        fixed = self.base[name] + self.now[name] + k
        if self.i is None or not self.per.get(name):
            return fixed
        return self.i * self.per[name] + fixed

    def take(self, name, n=1):
        value = self.at(name)
        self.now[name] += n
        return value

    @contextmanager
    def loop(self, engine, times, per):
        self.base.update(self.now)
        self.now.clear()
        with engine.Fori(0, times) as i:
            self.i, self.per = i, per
            yield i
            for name, n in self.now.items():
                assert n == per.get(name, 0), (name, n, per.get(name))
        self.i, self.per = None, {}
        self.now.clear()
        for name, n in per.items():
            self.base[name] += n * times


LN_TICKS = 15
RSQRT_BITS = float(0x5F3759DF - (1 << 22) - (1 << 30))
NODES_TWICE = {"F0": 6, "F1": 6, "F2": 8, "N0": 4, "N1": 4, "z1": 2, "z2": 2}


def build(nc, x, src, dst, edge_attr, w_self, w_neigh, b_self, w_edge, b_edge, eps, w1, b1, w2, b2, out):
    slot_of_node = nc.dram_tensor("slot_of_node", (N_NODES, 1), i32, kind="Internal").ap()
    x_slots = nc.dram_tensor("x_slots", (2 * EUNITS, P, UNIT * H), f32, kind="Internal").ap()
    table = [nc.dram_tensor(f"neigh_table{l}", (SLOTS, H), f32, kind="Internal").ap() for l in range(3)]
    edge_rows = nc.dram_tensor("edge_rows", (SLOTS, H), f32, kind="Internal").ap()

    with ExitStack() as ctx:
        def sb(name, shape, dt=f32):
            return ctx.enter_context(nc.sbuf_tensor(name, shape, dt))

        def sem(name):
            return ctx.enter_context(nc.semaphore(name))

        ident = sb("ident", [P, P])
        w_raw = sb("w_raw", [H, 5, H])
        WS = sb("WS", [K1, K1])
        WN = sb("WN", [K1, K1])
        WE = sb("WE", [K1, H])
        W1 = sb("W1", [K1, H])
        W1S = sb("W1S", [K1, H])
        W2 = sb("W2", [K1, H])
        eps1 = sb("eps1", [P, 1])
        rows_i = sb("rows_i", [ETILES, 3, P], i32)
        rows_f = sb("rows_f", [ETILES, 3, P])
        cont = sb("cont", [ETILES, P])
        x_idx = sb("x_idx", [P, 2 * ETILES], i32)
        end_idx = sb("end_idx", [P, ETILES, 2], i32)
        q_idx = sb("q_idx", [P, ETILES], i32)
        big = sb("big", [MAP_ROWS, N_NODES // MAP_ROWS], i32)
        iring = sb("iring", [P, 2, UNIT], i32)
        ering = sb("ering", [P, 2, UNIT, 2], i32)
        qring = sb("qring", [P, 2, UNIT], i32)
        xn = sb("xn", [P, 2, UNIT, H])
        x1n = sb("x1n", [P, 2, UNIT, H])
        z1 = sb("z1", [P, UNIT, K1])
        z2 = sb("z2", [P, UNIT, K1])
        ha = sb("ha", [K1, COLS])
        hb = sb("hb", [K1, COLS])
        ga = sb("ga", [K1, COLS])
        gb = sb("gb", [K1, COLS])
        state = sb("state", [K1, 2 * SLOTS])
        same = sb("same", [K1, SLOTS], bf16)
        xg = sb("xg", [P, 2, UNIT, H])
        G = sb("G", [P, 2, HALF, H])
        T = sb("T", [P, 2, HALF, H])
        S = sb("S", [K1, 2, COLS])
        rdeg = sb("rdeg", [P, ETILES])
        er = sb("er", [P, HALF, H])
        st = sb("st", [P, UNIT, 6])
        mean = sb("mean", [P, UNIT])
        diff = sb("diff", [P, UNIT])
        var = sb("var", [P, UNIT])
        rstd = sb("rstd", [P, UNIT])

        F = {f"F{k}": ctx.enter_context(nc.psum_tensor(f"F{k}", [P, 1024], f32)) for k in range(3)}
        Nb = {f"N{k}": ctx.enter_context(nc.psum_tensor(f"N{k}", [P, 512], f32)) for k in range(2)}

        full = {k: sem(f"{k}_full") for k in (*F, *Nb)}
        done = {k: sem(f"{k}_done") for k in (*F, *Nb)}
        z_full = {k: sem(f"{k}_full") for k in ("z1", "z2")}
        ln_tick = sem("ln_tick")
        x_in = [sem(f"x_in{u}") for u in range(2)]
        y_out = [sem(f"y_out{u}") for u in range(2)]
        xg_in = [sem(f"xg_in{u}") for u in range(2)]
        xg_out = [sem(f"xg_out{u}") for u in range(2)]
        zg_full = sem("zg_full")
        idx_copied = sem("idx_copied")
        map_in = [sem(f"map_in{u}") for u in range(2)]
        q_in = [sem(f"q_in{u}") for u in range(2)]
        q_copied = sem("q_copied")
        pool_order = sem("pool_order")
        g_zero = [sem(f"g_zero{u}") for u in range(2)]
        g_in = [sem(f"g_in{u}") for u in range(2)]
        scanned = sem("scanned")
        deg_done = sem("deg_done")
        t_full = sem("t_full")
        t_out = [sem(f"t_out{u}") for u in range(2)]
        loaded_w = sem("loaded_w")
        loaded_b = sem("loaded_b")
        loaded_rows = sem("loaded_rows")
        loaded_dst = sem("loaded_dst")
        consts_pool = sem("consts_pool")
        consts_dve = sem("consts_dve")
        weights_t = sem("weights_t")
        weights_sb = sem("weights_sb")
        rows_ready = sem("rows_ready")
        rows_t = sem("rows_t")
        idx_ready = sem("idx_ready")
        same_ready = sem("same_ready")
        dve_prep = sem("dve_prep")
        map_cleared = sem("map_cleared")
        edges_copied = sem("edges_copied")
        e_in = [sem(f"e_in{u}") for u in range(2)]
        state_copied = sem("state_copied")
        x1_tick = sem("x1_tick")
        h_mixed = sem("h_mixed")
        yo = [sem(f"yo{u}") for u in range(2)]

        def node_rows(t, pair):
            own = t[0:P * ROWS, :].rearrange("(p r) f -> p r f", p=P)
            return own[:, bass.ds(pair * UNIT, UNIT), :]

        def last_rows(t):
            return t[N_NODES - P * UNIT:N_NODES, :].rearrange("(p r) f -> p r f", p=P)

        def slot_rows(t, chunk):
            return t[bass.ds(chunk * COLS, COLS), :].rearrange("(t p) f -> p t f", p=P)

        block = ctx.enter_context(nc.Block())

        @block.sync
        def _(sp):
            t = Tally()
            for n, w in enumerate((w_self, w_neigh, w_edge, w1, w2)):
                sp.dma_start(w_raw[:, n, :], w).then_inc(loaded_w, 16)
            sp.dma_start(xn[:, 0], node_rows(x, 0)).then_inc(x_in[0], 16)
            sp.wait_ge(consts_dve, 1)
            cut = FULL_ROWS * P
            for k, (v, off) in enumerate(((src, 0), (dst, 0), (dst, 1))):
                sp.dma_start(rows_i[0:FULL_ROWS, k, :], v[off:off + cut].rearrange("(t p) -> t p", p=P))\
                    .then_inc(loaded_rows, 16)
                sp.dma_start(rows_i[FULL_ROWS:FULL_ROWS + 1, k, 0:REST - off],
                             v[cut + off:N_EDGES].rearrange("(t p) -> t p", t=1)).then_inc(loaded_rows, 16)
            sp.dma_start(slot_of_node.rearrange("(p r) a -> p (r a)", p=MAP_ROWS), big[:])\
                .then_inc(map_cleared, 16)
            sp.dma_start(xn[:, 1], node_rows(x, 1)).then_inc(x_in[1], 16)
            sp.wait_ge(consts_dve, 3)
            for m, b in ((WS, b_self), (WE, b_edge), (W1, b1), (W1S, b1), (W2, b2)):
                sp.dma_start(m[H:K1, 0:H], b.rearrange("(a f) -> a f", a=1)).then_inc(loaded_b, 16)
            sp.dma_start(eps1[:], eps.rearrange("(a f) -> a f", a=1).broadcast_to([P, 1])).then_inc(loaded_b, 16)
            dst_all = state[:, SLOTS:SLOTS + N_EDGES].bitcast(i32)
            dst_row = dst.rearrange("(a e) -> a e", a=1)
            sp.dma_start(dst_all[0:H, :], dst_row.broadcast_to([H, N_EDGES])).then_inc(loaded_dst, 16)
            sp.dma_start(dst_all[H:K1, :], dst_row).then_inc(loaded_dst, 16)
            sp.dma_start(edge_rows[0:N_EDGES, :].rearrange("(r s) f -> r (s f)", r=4 * 25),
                         edge_attr.rearrange("(r s) f -> r (s f)", r=4 * 25)).then_inc(edges_copied, 16)
            sp.wait_ge(consts_pool, 2)
            pad = SLOTS - N_EDGES
            sp.dma_start(edge_rows[N_EDGES:SLOTS, :].rearrange("(r s) f -> r s f", s=3),
                         G[0:pad // 3, 0, 0:3, :]).then_inc(edges_copied, 16)

            def nodes(pair, u, first, second, load, load_last=False, store_last=False):
                if second:
                    t.take("N0")
                if first:
                    t.take("N1")
                    n = t.take("N0")
                    if load or load_last:
                        sp.wait_ge(done["N0"], n + 1)
                        rows = last_rows(x) if load_last else node_rows(x, pair + 2)
                        sp.dma_start(xn[:, u], rows).then_inc(x_in[u], 16)
                if second:
                    sp.wait_ge(done["N1"], t.take("N1") + 1)
                    if store_last:
                        sp.wait_ge(y_out[0], 16 * (PAIRS // 2))
                        sp.wait_ge(y_out[1], 16 * (PAIRS // 2 - 1))
                    rows = last_rows(out) if store_last else node_rows(out, pair - 1)
                    sp.dma_start(rows, x1n[:, 1 - u]).then_inc(y_out[1 - u], 16)

            t.take("N0")
            nodes(0, 0, True, False, True)
            nodes(1, 1, True, True, True)
            with t.loop(sp, (PAIRS - 6) // 2, {"N0": 4, "N1": 4}) as i:
                for u in range(2):
                    nodes(2 * i + 2 + u, u, True, True, True)
            nodes(PAIRS - 4, 0, True, True, True)
            nodes(PAIRS - 3, 1, True, True, False, load_last=True)
            nodes(PAIRS - 2, 0, True, True, False)
            nodes(PAIRS - 1, 1, True, True, False)
            nodes(PAIRS, 0, False, True, False, store_last=True)

            t2 = Tally()
            with t2.loop(sp, EUNITS, {"u": 1}) as i:
                for u in range(2):
                    sp.wait_ge(xg_in[u], 16 * UNIT * t2.at("u"))
                    sp.dma_start(x_slots[bass.ds(2 * i + u, 1), :, :].rearrange("a p c -> (a p) c"),
                                 xg[:, u].rearrange("p t f -> p (t f)")).then_inc(xg_out[u], 16)
                t2.take("u")

            for l in range(3):
                with t.loop(sp, EUNITS, {"T": 2}) as i:
                    for u in range(2):
                        sp.wait_ge(t_full, t.take("T"))
                        sp.dma_start(slot_rows(table[l], 2 * i + u), T[:, u]).then_inc(t_out[u], 16)
            sp.wait_ge(t_out[0], 16 * 3 * EUNITS)
            sp.wait_ge(t_out[1], 16 * 3 * EUNITS)
            sp.wait_ge(xg_out[0], 16 * EUNITS)
            sp.wait_ge(xg_out[1], 16 * EUNITS)
            sp.wait_ge(edges_copied, 32)

            def last_loads(i, u):
                for k, j in ((0, i), (1, i + EUNITS)):
                    sp.dma_start(xg[:, 0, k * HALF:(k + 1) * HALF, :].rearrange("p t f -> p (t f)"),
                                 x_slots[bass.ds(j, 1), :, u * HALF * H:(u + 1) * HALF * H]
                                 .rearrange("a p c -> (a p) c")).then_inc(e_in[u], 16)
                sp.dma_start(T[:, 0], slot_rows(table[2], 2 * i + u)).then_inc(e_in[u], 16)
                sp.dma_start(er[:], slot_rows(edge_rows, 2 * i + u)).then_inc(e_in[u], 16)

            with t.loop(sp, EUNITS, {"N1": 4}) as i:
                for u in range(2):
                    sp.wait_ge(done["N1"], t.take("N1", 2))
                    last_loads(i, u)
            sp.wait_ge(yo[0], 16 * HALF * EUNITS)
            sp.wait_ge(yo[1], 16 * HALF * EUNITS)

        @block.gpsimd
        def _(pool):
            t = Tally()
            pool.memset(ident[:], 0.0).then_inc(consts_pool, 1)
            pool.memset(G[:], 0.0).then_inc(consts_pool, 1)
            pool.wait_ge(consts_pool, 2)
            pool.affine_select(out=ident[:], in_=ident[:], compare_op=ALU.not_equal, fill=1.0, base=0,
                               pattern=[[-1, P]], channel_multiplier=1).then_inc(consts_pool, 1)
            pool.iota(end_idx[:, :, 1], pattern=[[P, ETILES]], base=0, channel_multiplier=1)\
                .then_inc(consts_pool, 1)
            pool.wait_ge(consts_pool, 4)

            def order():
                pool.sem_inc(pool_order, 1)

            def copy_indices(to, of):
                pool.tensor_copy(to, of).then_inc(idx_copied, 1)
                pool.wait_ge(idx_copied, t.take("copy"))
                order()

            def map_unit(unit, u, first):
                if not first:
                    pool.wait_ge(map_in[u], 16 * UNIT * t.at("map", 0))
                    order()
                copy_indices(ering[:, u], end_idx[:, bass.ds(unit * UNIT, UNIT), :])
                for k in range(UNIT):
                    pool.indirect_dma_start(
                        out=slot_of_node, out_offset=bass.IndirectOffsetOnAxis(ap=ering[:, u, k, 0:1], axis=0),
                        in_=ering[:, u, k, 1:2], in_offset=None, bounds_check=N_NODES - 1,
                        oob_is_err=False).then_inc(map_in[u], 16)

            def map_lookup(unit, u):
                copy_indices(iring[:, u], x_idx[:, bass.ds(unit * UNIT, UNIT)])
                for k in range(UNIT):
                    pool.indirect_dma_start(
                        out=qring[:, u, k:k + 1], out_offset=None, in_=slot_of_node,
                        in_offset=bass.IndirectOffsetOnAxis(ap=iring[:, u, k:k + 1], axis=0),
                        bounds_check=N_NODES - 1, oob_is_err=False).then_inc(q_in[u], 16)

            def rows_unit(unit, u, first):
                if not first:
                    pool.wait_ge(xg_out[u], 16 * t.at("rows", 0))
                    order()
                    pool.wait_ge(zg_full, t.at("zg") - 2)
                    order()
                t.take("zg")
                copy_indices(iring[:, u], x_idx[:, bass.ds(unit * UNIT, UNIT)])
                for k in range(UNIT):
                    pool.indirect_dma_start(
                        out=xg[:, u, k, :], out_offset=None, in_=x,
                        in_offset=bass.IndirectOffsetOnAxis(ap=iring[:, u, k:k + 1], axis=0),
                        bounds_check=N_NODES - 1, oob_is_err=False).then_inc(xg_in[u], 16)

            pool.wait_ge(idx_ready, 3)
            pool.wait_ge(map_cleared, 16)
            map_unit(0, 0, True)
            map_unit(1, 1, True)
            t.take("map")
            with t.loop(pool, EUNITS // 2 - 1, {"copy": 2, "map": 1}) as i:
                for u in range(2):
                    map_unit(2 * i + 2 + u, u, False)
                t.take("map")
            for u in range(2):
                pool.wait_ge(map_in[u], 16 * UNIT * (EUNITS // 2))
            with t.loop(pool, EUNITS // 2, {"copy": 2, "q": 1}) as i:
                for u in range(2):
                    map_lookup(2 * i + u, u)
                for u in range(2):
                    pool.wait_ge(q_in[u], 16 * UNIT * t.at("q"))
                    order()
                    pool.tensor_copy(q_idx[:, bass.ds((2 * i + u) * UNIT, UNIT)], qring[:, u])\
                        .then_inc(q_copied, 1)
                t.take("q")
            rows_unit(0, 0, True)
            rows_unit(1, 1, True)
            t.take("rows")
            with t.loop(pool, EUNITS - 1, {"copy": 2, "rows": 1, "zg": 2}) as i:
                for u in range(2):
                    rows_unit(2 * i + 2 + u, u, False)
                t.take("rows")

            def neighbours(l, i, u):
                pool.wait_ge(g_zero[u], t.at("g"))
                order()
                copy_indices(iring[:, u, 0:HALF], q_idx[:, bass.ds((2 * i + u) * HALF, HALF)])
                for k in range(HALF):
                    pool.indirect_dma_start(
                        out=G[:, u, k, :], out_offset=None, in_=table[l],
                        in_offset=bass.IndirectOffsetOnAxis(ap=iring[:, u, k:k + 1], axis=0),
                        bounds_check=SLOTS - 1, oob_is_err=False).then_inc(g_in[u], 16)

            pool.wait_ge(q_copied, EUNITS)
            for u in range(2):
                pool.wait_ge(xg_in[u], 16 * UNIT * EUNITS)
            pool.wait_ge(edges_copied, 32)
            for l in range(2):
                for u in range(2):
                    pool.wait_ge(t_out[u], 16 * EUNITS * (l + 1))
                with t.loop(pool, EUNITS, {"copy": 2, "g": 1}) as i:
                    for u in range(2):
                        neighbours(l, i, u)
                    t.take("g")
            for u in range(2):
                pool.wait_ge(t_out[u], 16 * EUNITS * 3)
                pool.wait_ge(y_out[u], 16 * (PAIRS // 2))
            t.base["N1"] = 2 * PAIRS
            with t.loop(pool, EUNITS, {"copy": 4, "g": 1, "N1": 4}) as i:
                for u in range(2):
                    neighbours(2, i, u)
                    copy_indices(ering[:, u, 0:HALF], end_idx[:, bass.ds((2 * i + u) * HALF, HALF), :])
                    pool.wait_ge(done["N1"], t.take("N1", 2) + 2)
                    order()
                    for k in range(HALF):
                        pool.indirect_dma_start(
                            out=out, out_offset=bass.IndirectOffsetOnAxis(ap=ering[:, u, k, 0:1], axis=0),
                            in_=x1n[:, u, k, :], in_offset=None, bounds_check=N_NODES - 1,
                            oob_is_err=False).then_inc(yo[u], 16)
                t.take("g")

        @block.tensor
        def _(pe):
            t = Tally()

            def claim(name):
                pe.wait_ge(done[name], t.at(name))

            def fill(name, last):
                last.then_inc(full[name], 1)
                t.take(name)

            def transposes(name, z):
                for k in range(HALF):
                    last = nc.tensor.transpose(F[name][0:z.shape[2], k * P:(k + 1) * P], z[:, k, :], ident[:])
                fill(name, last)

            def wide(name, w, h, rows, more=()):
                for lo, n in ((0, 512), (512, COLS - 512)):
                    tiles = [k for k in range(HALF) if lo <= k * P < lo + n] if more else []
                    last = nc.tensor.matmul(F[name][0:rows, lo:lo + n], w, h[:, lo:lo + n] if not callable(h)
                                            else h(lo, n), start=True, stop=True)
                    for k in tiles:
                        last = nc.tensor.matmul(F[name][0:H, k * P:(k + 1) * P], more[k], ident[:],
                                                start=False, stop=True, skip_group_check=True)
                fill(name, last)

            def tall(name, h, w, width):
                for k in range(HALF):
                    last = nc.tensor.matmul(Nb[name][:, k * width:(k + 1) * width], h[:, k * P:(k + 1) * P], w,
                                            start=True, stop=True)
                fill(name, last)

            pe.wait_ge(consts_pool, 3)
            pe.wait_ge(loaded_w, 16 * 5)
            claim("F0")
            for n in range(5):
                last = nc.tensor.transpose(F["F0"][0:H, n * H:(n + 1) * H], w_raw[:, n, :],
                                           ident[0:H, 0:H])
            fill("F0", last)
            pe.wait_ge(rows_ready, 1)
            claim("N0")
            for k in range(3):
                last = nc.tensor.transpose(Nb["N0"][:, k * ETILES:(k + 1) * ETILES], rows_f[:, k, :],
                                           ident[0:ETILES, 0:ETILES])
            fill("N0", last)
            pe.wait_ge(weights_sb, 1)
            pe.wait_ge(loaded_b, 16 * 6)
            pe.wait_ge(consts_dve, 3)

            def nodes(first, second):
                if first:
                    pe.wait_ge(z_full["z1"], t.take("z1"))
                    claim("F0")
                    transposes("F0", z1[:, 0:HALF, :])
                    claim("F1")
                    transposes("F1", z1[:, HALF:UNIT, :])
                    claim("F0")
                    wide("F0", WS[:], ha, K1)
                    claim("F1")
                    wide("F1", WS[:], hb, K1)
                if second:
                    pe.wait_ge(z_full["z2"], t.take("z2"))
                    claim("F2")
                    transposes("F2", z2[:, 0:HALF, :])
                if first:
                    claim("F0")
                    wide("F0", WS[:], ha, K1)
                if second:
                    claim("F2")
                    wide("F2", W1S[:], ga, H)
                if first:
                    claim("F1")
                    wide("F1", WS[:], hb, K1)
                if second:
                    claim("F2")
                    transposes("F2", z2[:, HALF:UNIT, :])
                    claim("N0")
                    tall("N0", ga, W2[:], H)
                if first:
                    claim("F0")
                    claim("N1")
                    tall("N1", ha, WS[:, 0:H], H)
                if second:
                    claim("F2")
                    wide("F2", W1S[:], gb, H)
                if first:
                    claim("F1")
                    claim("N0")
                    tall("N0", hb, WS[:, 0:H], H)
                if second:
                    claim("F2")
                    claim("N1")
                    tall("N1", gb, W2[:], H)

            nodes(True, False)
            with t.loop(pe, (PAIRS - 2) // 2, NODES_TWICE):
                nodes(True, True)
                nodes(True, True)
            nodes(True, True)
            nodes(False, True)

            with t.loop(pe, EUNITS, {"F2": 4, "zg": 2}):
                for u in range(2):
                    pe.wait_ge(zg_full, t.take("zg"))
                    for half in range(2):
                        claim("F2")
                        transposes("F2", z1[:, half * HALF:(half + 1) * HALF, :])

            for l in range(3):
                def columns(side, c):
                    return lambda lo, n: state[:, bass.ds(side * SLOTS + c * COLS + lo, n)]

                pe.wait_ge(done["F2"], t.at("F2", 0) + 1)
                with t.loop(pe, EUNITS, {"F0": 2 * (l > 0), "N0": 2, "F1": 2 * (l < 2), "scan": 2, "T": 2,
                                         "g": int(l > 0)}) as i:
                    for u in range(2):
                        c = 2 * i + u
                        if l:
                            pe.wait_ge(g_in[u], 16 * HALF * t.at("g"))
                            claim("F0")
                            wide("F0", WS[:], columns(0, c), K1, [G[:, u, k, :] for k in range(HALF)])
                        pe.wait_ge(scanned, t.take("scan"))
                        claim("N0")
                        tall("N0", S[:, u], WN[:], K1)
                        if l < 2:
                            pe.wait_ge(t_full, t.take("T"))
                            claim("F1")
                            wide("F1", WS[:], columns(1, c), K1, [T[:, u, k, :] for k in range(HALF)])
                        else:
                            t.take("T")
                    t.take("g", int(l > 0))

            with t.loop(pe, EUNITS, {"F0": 2, "F1": 4, "F2": 4, "N0": 2, "N1": 4, "z2": 2, "hc": 2, "mix": 2,
                                     "e": 1}) as i:
                for u in range(2):
                    pe.wait_ge(state_copied, t.take("hc"))
                    claim("N0")
                    tall("N0", ha, WS[:, 0:H], H)
                    claim("N1")
                    tall("N1", hb, WS[:, 0:H], H)
                    pe.wait_ge(e_in[u], 16 * 4 * t.at("e"))
                    claim("F2")
                    transposes("F2", er[:, :, :])
                    pe.wait_ge(z_full["z2"], t.take("z2"))
                    claim("F0")
                    transposes("F0", z2[:, 0:HALF, :])
                    claim("F1")
                    transposes("F1", z2[:, HALF:UNIT, :])
                    claim("F2")
                    pe.wait_ge(done["F0"], t.at("F0"))
                    for lo, n in ((0, 512), (512, COLS - 512)):
                        nc.tensor.matmul(F["F2"][0:H, lo:lo + n], WE[:], ga[:, lo:lo + n], start=True, stop=False)
                        last = nc.tensor.matmul(F["F2"][0:H, lo:lo + n], ident[0:H, 0:H], ha[0:H, lo:lo + n],
                                                start=False, stop=True)
                    fill("F2", last)
                    pe.wait_ge(h_mixed, t.take("mix"))
                    claim("F1")
                    wide("F1", W1[:], gb, H)
                    claim("F1")
                    claim("N1")
                    tall("N1", gb, W2[:], H)
                t.take("e")

        @block.scalar
        def _(act):
            t = Tally()
            for name in F:
                act.sem_inc(done[name], 1)

            def drain(name, to, rows, relu=True):
                act.wait_ge(full[name], t.take(name))
                nc.scalar.activation(to, F[name][0:rows, 0:COLS], ACT.Relu if relu else ACT.Copy)\
                    .then_inc(done[name], 1)

            act.wait_ge(full["F0"], t.take("F0"))
            act.wait_ge(consts_dve, 3)
            for n, (m, w) in enumerate(((WS, 0), (WN, 1), (WE, 2), (W1, 3), (W2, 4))):
                last = nc.scalar.activation(m[0:H, 0:H], F["F0"][0:H, w * H:(w + 1) * H], ACT.Copy)
            last = nc.scalar.activation(W1S[0:H, :], F["F0"][0:H, 3 * H:4 * H], ACT.Copy)
            last.then_inc(done["F0"], 1)

            def nodes(first, second):
                if first:
                    drain("F0", ha[:], K1)
                    drain("F1", hb[:], K1)
                    drain("F0", ha[:], K1)
                    drain("F1", hb[:], K1)
                if second:
                    drain("F2", ga[:], K1)
                if first:
                    drain("F0", ha[:], K1)
                if second:
                    drain("F2", ga[0:H, :], H)
                if first:
                    drain("F1", hb[:], K1)
                if second:
                    drain("F2", gb[:], K1)
                    drain("F2", gb[0:H, :], H)

            nodes(True, False)
            with t.loop(act, (PAIRS - 2) // 2, {"F0": 6, "F1": 6, "F2": 8}):
                nodes(True, True)
                nodes(True, True)
            nodes(True, True)
            nodes(False, True)

            with t.loop(act, EUNITS, {"F2": 4}) as i:
                for k in range(4):
                    if k == 0:
                        act.wait_ge(same_ready, 1)
                    drain("F2", state[:, bass.ds((4 * i + k) * COLS, COLS)], K1)

            for l in range(3):
                with t.loop(act, EUNITS, {"F0": 2 * (l > 0), "F1": 2 * (l < 2)}) as i:
                    for u in range(2):
                        c = 2 * i + u
                        if l:
                            drain("F0", state[:, bass.ds(c * COLS, COLS)], K1)
                        if l < 2:
                            drain("F1", state[:, bass.ds(SLOTS + c * COLS, COLS)], K1)

            act.wait_ge(done["F0"], t.at("F0", 0) + 1)
            act.wait_ge(done["F1"], t.at("F1", 0) + 1)
            t.base["N1"] = 2 * PAIRS
            with t.loop(act, EUNITS, {"F0": 2, "F1": 4, "F2": 4, "N1": 4}) as i:
                for u in range(2):
                    c = 2 * i + u
                    act.wait_ge(done["N1"], t.take("N1", 2))
                    nc.scalar.activation(ha[:], state[:, bass.ds(c * COLS, COLS)], ACT.Copy)
                    nc.scalar.activation(hb[:], state[:, bass.ds(SLOTS + c * COLS, COLS)], ACT.Copy)\
                        .then_inc(state_copied, 1)
                    drain("F2", ga[0:H, :], H, relu=False)
                    drain("F0", ha[:], K1)
                    drain("F1", hb[:], K1)
                    drain("F2", ga[0:H, :], H)
                    drain("F1", gb[0:H, :], H)

        @block.vector
        def _(dve):
            t = Tally()
            for name in Nb:
                dve.sem_inc(done[name], 1)
            for u in range(2):
                dve.sem_inc(g_zero[u], 1)
            nc.vector.memset(rows_i[:, 0, :], 0)
            nc.vector.memset(rows_i[:, 1, :], BIG)
            nc.vector.memset(rows_i[:, 2, :], -1)
            nc.vector.memset(big[:], BIG).then_inc(consts_dve, 1)
            nc.vector.memset(WN[:], 0.0)
            nc.vector.memset(S[:], 0.0)
            nc.vector.memset(z1[:], 1.0)
            nc.vector.memset(z2[:], 1.0)
            nc.vector.memset(ga[:], 1.0)
            nc.vector.memset(gb[:], 1.0)
            nc.vector.memset(WS[:], 0.0)
            nc.vector.memset(same[:], 0.0).then_inc(consts_dve, 1)

            dve.wait_ge(consts_dve, 2)
            nc.vector.memset(WN[H:K1, H:K1], 1.0)
            nc.vector.memset(WS[H:K1, H:K1], 1.0).then_inc(consts_dve, 1)

            dve.wait_ge(done["F0"], 2)
            dve.wait_ge(loaded_b, 16 * 6)
            nc.vector.tensor_scalar(eps1[:], eps1[:], 1.0, None, ALU.add).then_inc(dve_prep, 1)
            dve.wait_ge(dve_prep, 1)
            nc.vector.tensor_scalar(W1S[0:H, :], W1S[0:H, :], eps1[0:H, :], None, ALU.mult).then_inc(weights_sb, 1)

            dve.wait_ge(loaded_rows, 16 * 6)
            nc.vector.tensor_copy(rows_f[:, 0, :], rows_i[:, 0, :])
            nc.vector.tensor_scalar(rows_f[:, 1, :], rows_i[:, 1, :], float(N_NODES - 1), None, ALU.min)
            nc.vector.tensor_tensor(cont[:], rows_i[:, 1, :], rows_i[:, 2, :], ALU.is_equal).then_inc(dve_prep, 1)
            dve.wait_ge(dve_prep, 2)
            nc.vector.tensor_scalar(cont[:], cont[:], float(BIG), None, ALU.mult).then_inc(dve_prep, 1)
            dve.wait_ge(dve_prep, 3)
            nc.vector.tensor_tensor(rows_f[:, 2, :], cont[:], rows_i[:, 1, :], ALU.add).then_inc(rows_ready, 1)
            dve.wait_ge(full["N0"], t.take("N0"))
            dve.wait_ge(consts_pool, 4)
            idx_t = Nb["N0"]
            nc.vector.tensor_copy(x_idx[:, 0:ETILES], idx_t[:, 0:ETILES]).then_inc(idx_ready, 1)
            nc.vector.tensor_copy(x_idx[:, ETILES:2 * ETILES], idx_t[:, ETILES:2 * ETILES]).then_inc(idx_ready, 1)
            nc.vector.tensor_copy(end_idx[:, :, 0], idx_t[:, 2 * ETILES:3 * ETILES]).then_inc(idx_ready, 1)
            dve.wait_ge(idx_ready, 3)
            dve.sem_inc(done["N0"], 1)
            dve.wait_ge(loaded_dst, 32)
            dst_all = state[:, SLOTS:SLOTS + N_EDGES].bitcast(i32)
            nc.vector.tensor_tensor(same[:, 1:N_EDGES], dst_all[:, 1:N_EDGES], dst_all[:, 0:N_EDGES - 1],
                                    ALU.is_equal).then_inc(same_ready, 1)

            def tick(last):
                last.then_inc(ln_tick, 1)
                dve.wait_ge(ln_tick, t.take("ln"))

            def layernorm(rows, z):
                for k in range(UNIT):
                    last = nc.vector.bn_stats(st[:, k, :], rows[:, k, :])
                tick(last)
                nc.vector.tensor_tensor(mean[:], st[:, :, 1], st[:, :, 4], ALU.add)
                nc.vector.tensor_tensor(diff[:], st[:, :, 1], st[:, :, 4], ALU.subtract)
                tick(nc.vector.tensor_tensor(var[:], st[:, :, 2], st[:, :, 5], ALU.add))
                nc.vector.tensor_scalar(mean[:], mean[:], 0.5, None, ALU.mult)
                tick(nc.vector.scalar_tensor_tensor(out=diff[:], in0=diff[:], scalar=-0.125, in1=diff[:],
                                                    op0=ALU.mult, op1=ALU.mult))
                tick(nc.vector.scalar_tensor_tensor(out=var[:], in0=var[:], scalar=-0.5 / H, in1=diff[:],
                                                    op0=ALU.mult, op1=ALU.add))
                tick(nc.vector.tensor_scalar(var[:], var[:], -0.5 * LN_EPS, None, ALU.add))
                tick(nc.vector.tensor_scalar(rstd[:].bitcast(i32), var[:].bitcast(i32), -0.5, RSQRT_BITS,
                                             ALU.mult, ALU.add))
                for _ in range(3):
                    tick(nc.vector.tensor_tensor(diff[:], var[:], rstd[:], ALU.mult))
                    tick(nc.vector.tensor_tensor(diff[:], diff[:], rstd[:], ALU.mult))
                    tick(nc.vector.scalar_tensor_tensor(out=rstd[:], in0=diff[:], scalar=1.5, in1=rstd[:],
                                                        op0=ALU.add, op1=ALU.mult))
                for k in range(UNIT):
                    last = nc.vector.tensor_scalar(z[:, k, 0:H], rows[:, k, :], mean[:, k:k + 1],
                                                   rstd[:, k:k + 1], ALU.subtract, ALU.mult)
                return last

            def add_rows(name, to, rows):
                dve.wait_ge(full[name], t.take(name))
                nc.vector.tensor_tensor(to, rows, Nb[name][:, 0:HALF * H].rearrange("p (t f) -> p t f", f=H),
                                        ALU.add).then_inc(done[name], 1)

            lo, hi = slice(0, HALF), slice(HALF, UNIT)

            def nodes(u, first, second, ahead, reused=True):
                if second:
                    dve.wait_ge(done["N0"], t.at("N0", 0) + 1)
                    layernorm(x1n[:, 1 - u], z2).then_inc(z_full["z2"], 1)
                if ahead:
                    dve.wait_ge(x_in[1 - u], 16 * t.take(f"x_in{1 - u}"))
                    dve.wait_ge(full["F1"], t.at("F1"))
                    layernorm(xn[:, 1 - u], z1).then_inc(z_full["z1"], 1)
                if first:
                    t.take("F1", 3)
                if second:
                    t.take("F2", 4)
                    add_rows("N0", x1n[:, 1 - u, lo], x1n[:, 1 - u, lo])
                if first:
                    if reused:
                        dve.wait_ge(y_out[u], 16 * t.at(f"y{u}", 0))
                    t.take(f"y{u}")
                    add_rows("N1", x1n[:, u, lo], xn[:, u, lo])
                    add_rows("N0", x1n[:, u, hi], xn[:, u, hi])
                if second:
                    add_rows("N1", x1n[:, 1 - u, hi], x1n[:, 1 - u, hi])

            dve.wait_ge(x_in[0], 16)
            t.take("x_in0")
            layernorm(xn[:, 0], z1).then_inc(z_full["z1"], 1)
            nodes(0, True, False, True, reused=False)
            nodes(1, True, True, True, reused=False)
            with t.loop(dve, (PAIRS - 4) // 2, {"F1": 6, "F2": 8, "N0": 4, "N1": 4, "ln": 4 * LN_TICKS,
                                                "x_in0": 1, "x_in1": 1, "y0": 1, "y1": 1}):
                nodes(0, True, True, True)
                nodes(1, True, True, True)
            nodes(0, True, True, True)
            nodes(1, True, True, False)
            nodes(0, False, True, False)

            with t.loop(dve, EUNITS, {"ln": 2 * LN_TICKS, "rows": 1, "F2": 4}):
                for u in range(2):
                    dve.wait_ge(xg_in[u], 16 * UNIT * t.at("rows"))
                    dve.wait_ge(full["F2"], t.at("F2", 0))
                    t.take("F2", 2)
                    layernorm(xg[:, u], z1).then_inc(zg_full, 1)
                t.take("rows")

            def scan(c, u, data):
                if not (isinstance(c, int) and c == 0):
                    dve.wait_ge(scanned, t.at("scan", 0))
                nc.vector.tensor_tensor_scan(S[:, u], same[:, bass.ds(c * COLS, COLS)], data,
                                             S[:, 1 - u, COLS - 1:COLS], ALU.mult, ALU.add)\
                    .then_inc(scanned, 1)
                t.take("scan")

            dve.wait_ge(same_ready, 1)
            dve.wait_ge(done["F2"], t.at("F2", 0) + 1)

            def messages(l, c, u, first):
                if l:
                    dve.wait_ge(done["F0"], t.take("F0") + 1)
                scan(c, u, state[:, bass.ds(c * COLS, COLS)])
                if l:
                    nc.vector.memset(G[:, u], 0.0).then_inc(g_zero[u], 1)
                dve.wait_ge(full["N0"], t.take("N0"))
                sums = Nb["N0"][:, 0:HALF * K1].rearrange("p (t f) -> p t f", f=K1)
                if l == 0:
                    nc.vector.reciprocal(rdeg[:, bass.ds(c * HALF, HALF)], sums[:, :, H]).then_inc(deg_done, 1)
                    dve.wait_ge(deg_done, t.take("deg"))
                if not first:
                    dve.wait_ge(t_out[u], 16 * t.at("t_out", 0))
                    dve.wait_ge(full["F1"], t.at("F1", 0) - 1)
                t.take("F1", int(l < 2))
                nc.vector.tensor_tensor(T[:, u], sums[:, :, 0:H],
                                        rdeg[:, bass.ds(c * HALF, HALF)].unsqueeze(2).broadcast_to([P, HALF, H]),
                                        ALU.mult).then_inc(t_full, 1)
                dve.wait_ge(t_full, t.take("T"))
                dve.sem_inc(done["N0"], 1)

            t.take("F0")
            t.take("F0", 3 * PAIRS)
            for l in range(3):
                per = {"scan": 2, "N0": 2, "T": 2, "t_out": 1, "deg": 2 * (l == 0), "F1": 2 * (l < 2),
                       "F0": 2 * (l > 0), "g": 0}
                start = 0
                if l == 0:
                    for u in range(2):
                        messages(l, u, u, True)
                    t.take("t_out")
                    start = 1
                with t.loop(dve, EUNITS - start, per) as i:
                    for u in range(2):
                        messages(l, 2 * i + 2 * start + u, u, False)
                    t.take("t_out")

            dve.wait_ge(y_out[0], 16 * (PAIRS // 2))
            dve.wait_ge(y_out[1], 16 * (PAIRS // 2))

            def last(c, u, first):
                dve.wait_ge(e_in[u], 16 * 4 * t.at("e"))
                add_rows("N0", xg[:, 0, lo], xg[:, 0, lo])
                add_rows("N1", xg[:, 0, hi], xg[:, 0, hi])
                dve.wait_ge(done["N1"], t.at("N1", 0) + 1)
                dve.wait_ge(g_in[u], 16 * HALF * (2 * EUNITS + t.at("e")))
                nc.vector.tensor_tensor(xg[:, 0, lo], xg[:, 0, lo], G[:, u], ALU.add)
                nc.vector.tensor_tensor(xg[:, 0, hi], xg[:, 0, hi], T[:, 0], ALU.add).then_inc(x1_tick, 1)
                dve.wait_ge(x1_tick, t.take("x1"))
                nc.vector.memset(G[:, u], 0.0).then_inc(g_zero[u], 1)
                layernorm(xg[:, 0], z2).then_inc(z_full["z2"], 1)
                dve.wait_ge(done["F2"], t.take("F2", 2) + 2)
                scan_rows(c, u)
                dve.wait_ge(done["F1"], t.take("F1", 2) + 1)
                dve.wait_ge(scanned, t.at("scan", 0))
                nc.vector.scalar_tensor_tensor(out=gb[0:H, :], in0=hb[0:H, :], scalar=eps1[0:H, :],
                                               in1=S[0:H, u], op0=ALU.mult, op1=ALU.add).then_inc(h_mixed, 1)
                if not first:
                    dve.wait_ge(yo[u], 16 * HALF * t.at("e", 0))
                add_rows("N1", x1n[:, u, lo], xg[:, 0, hi])

            def scan_rows(c, u):
                dve.wait_ge(scanned, t.at("scan", 0))
                nc.vector.tensor_tensor_scan(S[0:H, u], same[0:H, bass.ds(c * COLS, COLS)], ga[0:H, :],
                                             S[0:H, 1 - u, COLS - 1:COLS], ALU.mult, ALU.add)\
                    .then_inc(scanned, 1)
                t.take("scan")

            per = {"e": 1, "N0": 2, "N1": 4, "x1": 2, "ln": 2 * LN_TICKS, "F2": 4, "F1": 4, "scan": 2}
            for u in range(2):
                last(u, u, True)
            t.take("e")
            with t.loop(dve, EUNITS - 1, per) as i:
                for u in range(2):
                    last(2 * i + 2 + u, u, False)
                t.take("e")


_INS = ["x", "src", "dst", "edge_attr_96", "L0_gnn_W_self", "L0_gnn_W_neigh", "L0_gnn_b", "L1_gnn_W_edge",
        "L1_gnn_b_edge", "L1_gnn_eps", "L1_gnn_W1", "L1_gnn_b1", "L1_gnn_W2", "L1_gnn_b2"]


def kernel(**inputs):
    import concourse.bacc as bacc
    from concourse.bass_utils import run_bass_kernel_spmd

    nc = bacc.Bacc("TRN2", target_bir_lowering=False, num_devices=1)
    arrays, args = {}, []
    for name in _INS:
        a = np.ascontiguousarray(inputs[name])
        if a.ndim == 0:
            a = a.reshape(1)
        arrays["in_" + name] = a
        args.append(nc.dram_tensor("in_" + name, a.shape, mybir.dt.from_np(a.dtype), kind="ExternalInput").ap())
    out = nc.dram_tensor("out", (N_NODES, H), f32, kind="ExternalOutput").ap()
    (x, src, dst, edge_attr, w_self, w_neigh, b, w_edge, b_edge, eps, w1, b1, w2, b2) = args
    build(nc, x, src, dst, edge_attr, w_self, w_neigh, b, w_edge, b_edge, eps, w1, b1, w2, b2, out)
    return run_bass_kernel_spmd(nc, [arrays], core_ids=[0]).results[0]["out"]
```

```python
from collections import Counter
from contextlib import ExitStack, contextmanager

import numpy as np

import concourse.bass as bass
from concourse import mybir

N_NODES = 50000
N_EDGES = 12500
H = 96
LN_EPS = 1e-5

P = 128
LAST_ACT = range(5)
RING = 4
ACT_TILES = ((), (), (0, 1), (2, 3), (4, 5), (6, 7))
OWN_TILES = (8, 9)
HALF = 5
UNIT = 2 * HALF
COLS = HALF * P
K1 = H + 1
PAIRS = -(-N_NODES // (UNIT * P))
ROWS = N_NODES // (P * UNIT) * UNIT
SLOTS = -(-N_EDGES // (UNIT * P)) * UNIT * P
ETILES = SLOTS // P
EUNITS = ETILES // UNIT
CHUNKS = 2 * EUNITS
FULL_ROWS = N_EDGES // P
REST = N_EDGES - FULL_ROWS * P
MAP_ROWS = 80
BIG = 1 << 17

f32, bf16, i32 = mybir.dt.float32, mybir.dt.bfloat16, mybir.dt.int32
ALU = mybir.AluOpType
ACT = mybir.ActivationFunctionType


class Tally:

    def __init__(self):
        self.base, self.now, self.per, self.i = Counter(), Counter(), {}, None

    def at(self, name, k=1):
        fixed = self.base[name] + self.now[name] + k
        if self.i is None or not self.per.get(name):
            return fixed
        return self.i * self.per[name] + fixed

    def take(self, name, n=1):
        value = self.at(name)
        self.now[name] += n
        return value

    @contextmanager
    def loop(self, engine, times, per):
        self.base.update(self.now)
        self.now.clear()
        with engine.Fori(0, times) as i:
            self.i, self.per = i, per
            yield i
            for name, n in self.now.items():
                assert n == per.get(name, 0), (name, n, per.get(name))
        self.i, self.per = None, {}
        self.now.clear()
        for name, n in per.items():
            self.base[name] += n * times


LN_TICKS = 12
RSQRT_MAGIC = float(0x5F1FFFF9 - (1 << 22) - (1 << 30))
RSQRT_K, RSQRT_C = 0.703952253, 0.703952253 * 2.38924456
N1_LAST = 2 * PAIRS
F2_LAST = 2 * PAIRS + 4 * EUNITS
NODES_TWICE = {"F0": 6, "F1": 10, "F2": 4, "N0": 4, "N1": 4, "z1": 2, "z2": 2}


def build(nc, x, src, dst, edge_attr, w_self, w_neigh, b_self, w_edge, b_edge, eps, w1, b1, w2, b2, out):
    slot_of_node = nc.dram_tensor("slot_of_node", (N_NODES, 1), i32, kind="Internal").ap()
    x_slots = nc.dram_tensor("x_slots", (2 * EUNITS, P, UNIT * H), f32, kind="Internal").ap()
    table = [nc.dram_tensor(f"neigh_table{l}", (SLOTS, H), f32, kind="Internal").ap() for l in range(3)]
    edge_rows = nc.dram_tensor("edge_rows", (SLOTS, H), f32, kind="Internal").ap()

    with ExitStack() as ctx:
        def sb(name, shape, dt=f32):
            return ctx.enter_context(nc.sbuf_tensor(name, shape, dt))

        def sem(name):
            return ctx.enter_context(nc.semaphore(name))

        ident = sb("ident", [P, P])
        w_raw = sb("w_raw", [H, 5, H])
        WS = sb("WS", [K1, K1])
        WN = sb("WN", [K1, K1])
        WE = sb("WE", [K1, H])
        W1 = sb("W1", [K1, H])
        W1S = sb("W1S", [K1, H])
        W2 = sb("W2", [K1, H])
        eps1 = sb("eps1", [P, 1])
        rows_i = sb("rows_i", [ETILES, 3, P], i32)
        rows_f = sb("rows_f", [ETILES, 3, P])
        cont = sb("cont", [ETILES, P])
        x_idx = sb("x_idx", [P, 2 * ETILES], i32)
        end_idx = sb("end_idx", [P, ETILES, 2], i32)
        q_idx = sb("q_idx", [P, ETILES], i32)
        big = sb("big", [MAP_ROWS, N_NODES // MAP_ROWS], i32)
        iring = sb("iring", [P, 2, UNIT], i32)
        ering = sb("ering", [P, 2, UNIT, 2], i32)
        qring = sb("qring", [P, 2, UNIT], i32)
        R = sb("R", [P, RING, UNIT, H])
        z1 = sb("z1", [P, UNIT, K1])
        z2 = sb("z2", [P, UNIT, K1])
        ha = sb("ha", [K1, COLS])
        hb = sb("hb", [K1, COLS])
        ga = sb("ga", [K1, COLS])
        gb = sb("gb", [K1, COLS])
        state = sb("state", [K1, 2 * SLOTS])
        same = sb("same", [K1, SLOTS], bf16)
        xg = sb("xg", [P, 2, UNIT, H])
        G = sb("G", [P, 2, HALF, H])
        T = sb("T", [P, 2, HALF, H])
        S = sb("S", [K1, 2, COLS])
        rdeg = sb("rdeg", [P, ETILES])
        er = sb("er", [P, 2, HALF, H])
        st = sb("st", [P, 2 * UNIT, 6])
        mean = sb("mean", [P, 2 * UNIT])
        diff = sb("diff", [P, 2 * UNIT])
        var = sb("var", [P, 2 * UNIT])
        rstd = sb("rstd", [P, 2 * UNIT])
        shift = sb("shift", [P, UNIT])

        F = {f"F{k}": ctx.enter_context(nc.psum_tensor(f"F{k}", [P, 1024], f32)) for k in range(3)}
        Nb = {f"N{k}": ctx.enter_context(nc.psum_tensor(f"N{k}", [P, 512], f32)) for k in range(2)}

        full = {k: sem(f"{k}_full") for k in (*F, *Nb)}
        done = {k: sem(f"{k}_done") for k in (*F, *Nb)}
        z_full = {k: sem(f"{k}_full") for k in ("z1", "z2")}
        z2_act = sem("z2_act")
        shift_ready = sem("shift_ready")
        ln_tick = sem("ln_tick")
        x_in = [sem(f"x_in{b}") for b in range(RING)]
        y_out = [sem(f"y_out{b}") for b in range(RING)]
        xg_in = [sem(f"xg_in{u}") for u in range(2)]
        xg_out = [sem(f"xg_out{u}") for u in range(2)]
        zg_full = sem("zg_full")
        idx_copied = sem("idx_copied")
        map_in = [sem(f"map_in{u}") for u in range(2)]
        q_in = [sem(f"q_in{u}") for u in range(2)]
        q_copied = sem("q_copied")
        pool_order = sem("pool_order")
        act_order = sem("act_order")
        g_zero = [sem(f"g_zero{u}") for u in range(2)]
        g_in = [sem(f"g_in{u}") for u in range(2)]
        scanned = sem("scanned")
        deg_done = sem("deg_done")
        t_full = sem("t_full")
        t_out = [sem(f"t_out{u}") for u in range(2)]
        loaded_w = sem("loaded_w")
        loaded_b = sem("loaded_b")
        loaded_rows = sem("loaded_rows")
        loaded_dst = sem("loaded_dst")
        consts_pool = sem("consts_pool")
        consts_dve = sem("consts_dve")
        weights_t = sem("weights_t")
        weights_sb = sem("weights_sb")
        rows_ready = sem("rows_ready")
        rows_t = sem("rows_t")
        idx_ready = sem("idx_ready")
        same_ready = sem("same_ready")
        dve_prep = sem("dve_prep")
        map_cleared = sem("map_cleared")
        edges_copied = sem("edges_copied")
        e_in = [sem(f"e_in{u}") for u in range(2)]
        state_copied = sem("state_copied")
        h_mixed = sem("h_mixed")
        yo = [sem(f"yo{u}") for u in range(2)]

        def node_rows(t, pair):
            own = t[0:P * ROWS, :].rearrange("(p r) f -> p r f", p=P)
            return own[:, bass.ds(pair * UNIT, UNIT), :]

        def last_rows(t):
            return t[N_NODES - P * UNIT:N_NODES, :].rearrange("(p r) f -> p r f", p=P)

        def slot_rows(t, chunk):
            return t[bass.ds(chunk * COLS, COLS), :].rearrange("(t p) f -> p t f", p=P)

        block = ctx.enter_context(nc.Block())

        @block.sync
        def _(sp):
            t = Tally()
            for n, w in enumerate((w_self, w_neigh, w_edge, w1, w2)):
                sp.dma_start(w_raw[:, n, :], w).then_inc(loaded_w, 16)
            sp.dma_start(R[:, 0], node_rows(x, 0)).then_inc(x_in[0], 16)
            sp.wait_ge(consts_dve, 1)
            cut = FULL_ROWS * P
            for k, (v, off) in enumerate(((src, 0), (dst, 0), (dst, 1))):
                sp.dma_start(rows_i[0:FULL_ROWS, k, :], v[off:off + cut].rearrange("(t p) -> t p", p=P))\
                    .then_inc(loaded_rows, 16)
                sp.dma_start(rows_i[FULL_ROWS:FULL_ROWS + 1, k, 0:REST - off],
                             v[cut + off:N_EDGES].rearrange("(t p) -> t p", t=1)).then_inc(loaded_rows, 16)
            sp.dma_start(slot_of_node.rearrange("(p r) a -> p (r a)", p=MAP_ROWS), big[:])\
                .then_inc(map_cleared, 16)
            for q in range(1, RING):
                sp.dma_start(R[:, q], node_rows(x, q)).then_inc(x_in[q], 16)
            sp.wait_ge(consts_dve, 3)
            for m, b in ((WS, b_self), (WE, b_edge), (W1, b1), (W1S, b1), (W2, b2)):
                sp.dma_start(m[H:K1, 0:H], b.rearrange("(a f) -> a f", a=1)).then_inc(loaded_b, 16)
            sp.dma_start(eps1[:], eps.rearrange("(a f) -> a f", a=1).broadcast_to([P, 1])).then_inc(loaded_b, 16)
            dst_all = state[:, SLOTS:SLOTS + N_EDGES].bitcast(i32)
            dst_row = dst.rearrange("(a e) -> a e", a=1)
            sp.dma_start(dst_all[0:H, :], dst_row.broadcast_to([H, N_EDGES])).then_inc(loaded_dst, 16)
            sp.dma_start(dst_all[H:K1, :], dst_row).then_inc(loaded_dst, 16)
            sp.dma_start(edge_rows[0:N_EDGES, :].rearrange("(r s) f -> r (s f)", r=4 * 25),
                         edge_attr.rearrange("(r s) f -> r (s f)", r=4 * 25)).then_inc(edges_copied, 16)
            sp.wait_ge(consts_pool, 2)
            pad = SLOTS - N_EDGES
            sp.dma_start(edge_rows[N_EDGES:SLOTS, :].rearrange("(r s) f -> r s f", s=3),
                         G[0:pad // 3, 0, 0:3, :]).then_inc(edges_copied, 16)

            def nodes(i, k, load=True, sage=True, last=False):
                if load:
                    sp.wait_ge(y_out[k], 16 * (i + 1))
                    rows = last_rows(x) if last else node_rows(x, 4 * i + 4 + k)
                    sp.dma_start(R[:, k], rows).then_inc(x_in[k], 16)
                t.take("N1", int(sage))
                sp.wait_ge(done["N1"], t.take("N1") + 1)
                b = (k + 1) % RING
                if last and not load:
                    for j in range(RING):
                        sp.wait_ge(y_out[j], 16 * (PAIRS // RING - (j == b)))
                rows = last_rows(out) if last and not load else node_rows(out, 4 * i + 1 + k)
                sp.dma_start(rows, R[:, b]).then_inc(y_out[b], 16)

            t.take("N1")
            nodes(-1, 3, load=False)
            TURNS = PAIRS // RING - 1
            with t.loop(sp, TURNS - 1, {"N1": 8}) as i:
                for k in range(RING):
                    nodes(i, k)
            for k in range(RING):
                nodes(TURNS - 1, k, last=k == RING - 1)
            nodes(TURNS, 0, load=False)
            nodes(TURNS, 1, load=False)
            nodes(TURNS, 2, load=False, sage=False, last=True)

            t2 = Tally()
            with t2.loop(sp, EUNITS, {"u": 1}) as i:
                for u in range(2):
                    sp.wait_ge(xg_in[u], 16 * UNIT * t2.at("u"))
                    sp.dma_start(x_slots[bass.ds(2 * i + u, 1), :, :].rearrange("a p c -> (a p) c"),
                                 xg[:, u].rearrange("p t f -> p (t f)")).then_inc(xg_out[u], 16)
                t2.take("u")

            for l in range(3):
                with t.loop(sp, EUNITS, {"T": 2}) as i:
                    for u in range(2):
                        sp.wait_ge(t_full, t.take("T"))
                        sp.dma_start(slot_rows(table[l], 2 * i + u), T[:, u]).then_inc(t_out[u], 16)
            sp.wait_ge(t_out[0], 16 * 3 * EUNITS)
            sp.wait_ge(t_out[1], 16 * 3 * EUNITS)
            sp.wait_ge(xg_out[0], 16 * EUNITS)
            sp.wait_ge(xg_out[1], 16 * EUNITS)
            sp.wait_ge(edges_copied, 32)

            def last_loads(turn, u, n1=None):
                if n1 is not None:
                    sp.wait_ge(done["N1"], n1)
                for k, j in ((0, turn), (1, turn + EUNITS)):
                    sp.dma_start(xg[:, u, k * HALF:(k + 1) * HALF, :].rearrange("p t f -> p (t f)"),
                                 x_slots[bass.ds(j, 1), :, u * HALF * H:(u + 1) * HALF * H]
                                 .rearrange("a p c -> (a p) c")).then_inc(e_in[u], 16)
                sp.dma_start(T[:, u], slot_rows(table[2], 2 * turn + u)).then_inc(e_in[u], 16)
                if n1 is not None:
                    sp.wait_ge(full["F2"], F2_LAST + 1 + 2 * (2 * turn + u - 2))
                sp.dma_start(er[:, u], slot_rows(edge_rows, 2 * turn + u)).then_inc(e_in[u], 16)

            last_loads(0, 0)
            last_loads(0, 1)
            last_loads(1, 0, N1_LAST + 2)
            last_loads(1, 1, N1_LAST + 1 + 2)
            with t.loop(sp, EUNITS - 2, {}) as i:
                for u in range(2):
                    last_loads(i + 2, u, N1_LAST + 1 + 2 * (2 * i + 2 + u))
            sp.wait_ge(yo[0], 16 * HALF * EUNITS)
            sp.wait_ge(yo[1], 16 * HALF * EUNITS)

        @block.gpsimd
        def _(pool):
            t = Tally()
            pool.memset(ident[:], 0.0).then_inc(consts_pool, 1)
            pool.memset(G[:], 0.0).then_inc(consts_pool, 1)
            pool.wait_ge(consts_pool, 2)
            pool.affine_select(out=ident[:], in_=ident[:], compare_op=ALU.not_equal, fill=1.0, base=0,
                               pattern=[[-1, P]], channel_multiplier=1).then_inc(consts_pool, 1)
            pool.iota(end_idx[:, :, 1], pattern=[[P, ETILES]], base=0, channel_multiplier=1)\
                .then_inc(consts_pool, 1)
            pool.wait_ge(consts_pool, 4)

            def order():
                pool.sem_inc(pool_order, 1)

            def copy_indices(to, of):
                pool.tensor_copy(to, of).then_inc(idx_copied, 1)
                pool.wait_ge(idx_copied, t.take("copy"))
                order()

            def map_unit(unit, u, first):
                if not first:
                    pool.wait_ge(map_in[u], 16 * UNIT * t.at("map", 0))
                    order()
                copy_indices(ering[:, u], end_idx[:, bass.ds(unit * UNIT, UNIT), :])
                for k in range(UNIT):
                    pool.indirect_dma_start(
                        out=slot_of_node, out_offset=bass.IndirectOffsetOnAxis(ap=ering[:, u, k, 0:1], axis=0),
                        in_=ering[:, u, k, 1:2], in_offset=None, bounds_check=N_NODES - 1,
                        oob_is_err=False).then_inc(map_in[u], 16)

            def map_lookup(unit, u):
                copy_indices(iring[:, u], x_idx[:, bass.ds(unit * UNIT, UNIT)])
                for k in range(UNIT):
                    pool.indirect_dma_start(
                        out=qring[:, u, k:k + 1], out_offset=None, in_=slot_of_node,
                        in_offset=bass.IndirectOffsetOnAxis(ap=iring[:, u, k:k + 1], axis=0),
                        bounds_check=N_NODES - 1, oob_is_err=False).then_inc(q_in[u], 16)

            def rows_unit(unit, u, first):
                if not first:
                    pool.wait_ge(xg_out[u], 16 * t.at("rows", 0))
                    order()
                    pool.wait_ge(zg_full, t.at("zg") - 2)
                    order()
                t.take("zg")
                copy_indices(iring[:, u], x_idx[:, bass.ds(unit * UNIT, UNIT)])
                for k in range(UNIT):
                    pool.indirect_dma_start(
                        out=xg[:, u, k, :], out_offset=None, in_=x,
                        in_offset=bass.IndirectOffsetOnAxis(ap=iring[:, u, k:k + 1], axis=0),
                        bounds_check=N_NODES - 1, oob_is_err=False).then_inc(xg_in[u], 16)

            pool.wait_ge(idx_ready, 3)
            pool.wait_ge(map_cleared, 16)
            map_unit(0, 0, True)
            map_unit(1, 1, True)
            t.take("map")
            with t.loop(pool, EUNITS // 2 - 1, {"copy": 2, "map": 1}) as i:
                for u in range(2):
                    map_unit(2 * i + 2 + u, u, False)
                t.take("map")
            for u in range(2):
                pool.wait_ge(map_in[u], 16 * UNIT * (EUNITS // 2))
            with t.loop(pool, EUNITS // 2, {"copy": 2, "q": 1}) as i:
                for u in range(2):
                    map_lookup(2 * i + u, u)
                for u in range(2):
                    pool.wait_ge(q_in[u], 16 * UNIT * t.at("q"))
                    order()
                    pool.tensor_copy(q_idx[:, bass.ds((2 * i + u) * UNIT, UNIT)], qring[:, u])\
                        .then_inc(q_copied, 1)
                t.take("q")
            rows_unit(0, 0, True)
            rows_unit(1, 1, True)
            t.take("rows")
            with t.loop(pool, EUNITS - 1, {"copy": 2, "rows": 1, "zg": 2}) as i:
                for u in range(2):
                    rows_unit(2 * i + 2 + u, u, False)
                t.take("rows")

            def neighbours(l, i, u, back=0):
                pool.wait_ge(g_zero[u], t.at("g", 1 + back))
                order()
                copy_indices(iring[:, u, 0:HALF], q_idx[:, bass.ds((2 * i + u) * HALF, HALF)])
                for k in range(HALF):
                    pool.indirect_dma_start(
                        out=G[:, u, k, :], out_offset=None, in_=table[l],
                        in_offset=bass.IndirectOffsetOnAxis(ap=iring[:, u, k:k + 1], axis=0),
                        bounds_check=SLOTS - 1, oob_is_err=False).then_inc(g_in[u], 16)

            pool.wait_ge(q_copied, EUNITS)
            for u in range(2):
                pool.wait_ge(xg_in[u], 16 * UNIT * EUNITS)
            pool.wait_ge(edges_copied, 32)
            for l in range(2):
                for u in range(2):
                    pool.wait_ge(t_out[u], 16 * EUNITS * (l + 1))
                with t.loop(pool, EUNITS, {"copy": 2, "g": 1}) as i:
                    for u in range(2):
                        neighbours(l, i, u)
                    t.take("g")
            for b in range(RING):
                pool.wait_ge(y_out[b], 16 * (PAIRS // RING))
            for u in range(2):
                pool.wait_ge(t_out[u], 16 * EUNITS * 3)

            def scatter(turn, u, first=False, final=False):
                if not first:
                    pool.wait_ge(yo[u], 16 * HALF * turn)
                    order()
                copy_indices(ering[:, u, 0:HALF], end_idx[:, bass.ds((2 * turn + u) * HALF, HALF), :])
                pool.wait_ge(done["N1"], N1_LAST + 1 + 2 * (2 * turn + u) + (2 if final else 3))
                order()
                for k in range(HALF):
                    pool.indirect_dma_start(
                        out=out, out_offset=bass.IndirectOffsetOnAxis(ap=ering[:, u, k, 0:1], axis=0),
                        in_=R[:, 2 + u, k, :], in_offset=None, bounds_check=N_NODES - 1,
                        oob_is_err=False).then_inc(yo[u], 16)

            neighbours(2, 0, 0)
            neighbours(2, 0, 1)
            t.take("g")
            neighbours(2, 1, 0)

            def turn_round(turn, first=False):
                t.take("g")
                neighbours(2, turn + 1, 1, -1)
                scatter(turn, 0, first)
                neighbours(2, turn + 2, 0)
                scatter(turn, 1, first)

            turn_round(0, True)
            with t.loop(pool, EUNITS - 3, {"copy": 4, "g": 1}) as i:
                turn_round(i + 1)
            t.take("g")
            neighbours(2, EUNITS - 1, 1, -1)
            scatter(EUNITS - 2, 0)
            scatter(EUNITS - 2, 1)
            scatter(EUNITS - 1, 0)
            scatter(EUNITS - 1, 1, final=True)

        @block.tensor
        def _(pe):
            t = Tally()

            def claim(name):
                pe.wait_ge(done[name], t.at(name))

            def fill(name, last):
                last.then_inc(full[name], 1)
                t.take(name)

            def transposes(name, z):
                for k in range(HALF):
                    last = nc.tensor.transpose(F[name][0:z.shape[2], k * P:(k + 1) * P], z[:, k, :], ident[:])
                fill(name, last)

            def wide(name, w, h, rows, more=()):
                for lo, n in ((0, 512), (512, COLS - 512)):
                    tiles = [k for k in range(HALF) if lo <= k * P < lo + n] if more else []
                    last = nc.tensor.matmul(F[name][0:rows, lo:lo + n], w, h[:, lo:lo + n] if not callable(h)
                                            else h(lo, n), start=True, stop=True)
                    for k in tiles:
                        last = nc.tensor.matmul(F[name][0:H, k * P:(k + 1) * P], more[k], ident[:],
                                                start=False, stop=True, skip_group_check=True)
                fill(name, last)

            def tall(name, h, w, width, rows=None):
                if rows is not None:
                    nc.tensor.matmul(Nb[name][:, 0:HALF * width], ident[:], rows.rearrange("p t f -> p (t f)"),
                                     start=True, stop=True)
                for k in range(HALF):
                    last = nc.tensor.matmul(Nb[name][:, k * width:(k + 1) * width], h[:, k * P:(k + 1) * P], w,
                                            start=rows is None, stop=True, skip_group_check=rows is not None)
                fill(name, last)

            pe.wait_ge(consts_pool, 3)
            pe.wait_ge(loaded_w, 16 * 5)
            claim("F0")
            for n in range(5):
                last = nc.tensor.transpose(F["F0"][0:H, n * H:(n + 1) * H], w_raw[:, n, :],
                                           ident[0:H, 0:H])
            fill("F0", last)
            pe.wait_ge(rows_ready, 1)
            claim("N0")
            for k in range(3):
                last = nc.tensor.transpose(Nb["N0"][:, k * ETILES:(k + 1) * ETILES], rows_f[:, k, :],
                                           ident[0:ETILES, 0:ETILES])
            fill("N0", last)
            pe.wait_ge(weights_sb, 1)
            pe.wait_ge(loaded_b, 16 * 6)
            pe.wait_ge(consts_dve, 3)

            def nodes(first, second):
                if first:
                    pe.wait_ge(z_full["z1"], t.take("z1"))
                    claim("F0")
                    transposes("F0", z1[:, 0:HALF, :])
                    claim("F1")
                    transposes("F1", z1[:, HALF:UNIT, :])
                    for _ in range(2):
                        claim("F0")
                        wide("F0", WS[:], ha, K1)
                        claim("F1")
                        wide("F1", WS[:], hb, K1)
                    claim("F0")
                    claim("N0")
                    tall("N0", ha, WS[:, 0:H], H)
                if second:
                    pe.wait_ge(z2_act, t.at("z2"))
                    pe.wait_ge(z_full["z2"], t.at("z2"))
                    t.take("z2")
                    claim("F2")
                    transposes("F2", z2[:, 0:HALF, :])
                claim("F1")
                if first:
                    claim("N1")
                    tall("N1", hb, WS[:, 0:H], H)
                if second:
                    transposes("F1", z2[:, HALF:UNIT, :])
                    claim("F2")
                    wide("F2", W1S[:], ga, H)
                    claim("F1")
                    wide("F1", W1S[:], gb, H)
                    claim("F2")
                    claim("N0")
                    tall("N0", ga, W2[:], H)
                    claim("F1")
                    claim("N1")
                    tall("N1", gb, W2[:], H)

            nodes(True, False)
            with t.loop(pe, (PAIRS - 2) // 2, NODES_TWICE):
                nodes(True, True)
                nodes(True, True)
            nodes(True, True)
            nodes(False, True)

            with t.loop(pe, EUNITS, {"F2": 4, "zg": 2}):
                for u in range(2):
                    pe.wait_ge(zg_full, t.take("zg"))
                    for half in range(2):
                        claim("F2")
                        transposes("F2", z1[:, half * HALF:(half + 1) * HALF, :])

            def columns(side, c):
                return lambda lo, n: state[:, bass.ds(side * SLOTS + c * COLS + lo, n)]

            for l in range(3):
                pe.wait_ge(done["F2"], t.at("F2", 0) + 1)
                with t.loop(pe, EUNITS, {"F0": 2 * (l > 0), "N0": 2, "F1": 2 * (l < 2), "scan": 2, "T": 2,
                                         "g": int(l > 0)}) as i:
                    for u in range(2):
                        c = 2 * i + u
                        if l:
                            pe.wait_ge(g_in[u], 16 * HALF * t.at("g"))
                            claim("F0")
                            wide("F0", WS[:], columns(0, c), K1, [G[:, u, k, :] for k in range(HALF)])
                        pe.wait_ge(scanned, t.take("scan"))
                        claim("N0")
                        tall("N0", S[:, u], WN[:], K1)
                        if l < 2:
                            pe.wait_ge(t_full, t.take("T"))
                            claim("F1")
                            wide("F1", WS[:], columns(1, c), K1, [T[:, u, k, :] for k in range(HALF)])
                        else:
                            t.take("T")
                    t.take("g", int(l > 0))

            def last_step(turn, u, a, b, c):
                if a:
                    pe.wait_ge(state_copied, t.take("hc"))
                    pe.wait_ge(g_in[u], 16 * HALF * (2 * EUNITS + turn + 1))
                    claim("N0")
                    tall("N0", ha, WS[:, 0:H], H, G[:, u])
                if c:
                    claim("F1")
                    claim("N1")
                    tall("N1", gb, W2[:], H)
                if a:
                    pe.wait_ge(e_in[u], 16 * 4 * (turn + 1))
                    claim("N1")
                    tall("N1", hb, WS[:, 0:H], H, T[:, u])
                if b:
                    pe.wait_ge(z2_act, t.take("z2"))
                    pe.wait_ge(z_full["z2"], t.at("z2", 0))
                    claim("F0")
                    transposes("F0", z2[:, 0:HALF, :])
                    claim("F1")
                    transposes("F1", z2[:, HALF:UNIT, :])
                    claim("F2")
                    pe.wait_ge(done["F0"], t.at("F0"))
                    h = columns(0, 2 * turn + u - 1)
                    for lo, n in ((0, 512), (512, COLS - 512)):
                        nc.tensor.matmul(F["F2"][0:H, lo:lo + n], WE[:], ga[:, lo:lo + n], start=True, stop=False)
                        last = nc.tensor.matmul(F["F2"][0:H, lo:lo + n], ident[0:K1, 0:H], h(lo, n),
                                                start=False, stop=True)
                    fill("F2", last)
                if a:
                    claim("F2")
                    transposes("F2", er[:, u])
                if b:
                    pe.wait_ge(h_mixed, t.take("mix"))
                    claim("F1")
                    wide("F1", W1[:], gb, H)

            for turn in range(2):
                for u in range(2):
                    last_step(turn, u, True, turn + u > 0, turn > 0)
            with t.loop(pe, EUNITS - 2, {"F0": 2, "F1": 4, "F2": 4, "N0": 2, "N1": 4, "z2": 2, "hc": 2,
                                         "mix": 2}) as i:
                for u in range(2):
                    last_step(i + 2, u, True, True, True)
            last_step(EUNITS, 0, False, True, True)
            last_step(EUNITS, 1, False, False, True)

        @block.scalar
        def _(act):
            t = Tally()
            for name in F:
                act.sem_inc(done[name], 1)

            def drain(name, to, rows, relu=True, order=False):
                act.wait_ge(full[name], t.take(name))
                if order:
                    act.sem_inc(act_order, 1)
                nc.scalar.activation(to, F[name][0:rows, 0:COLS], ACT.Relu if relu else ACT.Copy)\
                    .then_inc(done[name], 1)

            act.wait_ge(full["F0"], t.take("F0"))
            act.wait_ge(consts_dve, 3)
            for n, (m, w) in enumerate(((WS, 0), (WN, 1), (WE, 2), (W1, 3), (W2, 4))):
                last = nc.scalar.activation(m[0:H, 0:H], F["F0"][0:H, w * H:(w + 1) * H], ACT.Copy)
            last = nc.scalar.activation(W1S[0:H, :], F["F0"][0:H, 3 * H:4 * H], ACT.Copy)
            last.then_inc(done["F0"], 1)

            def normalise(rows, tiles):
                for k in tiles:
                    last = nc.scalar.activation(z2[:, k, 0:H], rows[:, k, :], ACT.Identity,
                                                bias=shift[:, k:k + 1], scale=rstd[:, k:k + 1])
                return last

            def nodes(b, first, second):
                for n, tiles in enumerate(ACT_TILES):
                    if first:
                        name, to = (("F0", ha), ("F1", hb))[n % 2]
                        drain(name, to[:], K1)
                    if second and tiles:
                        if not any(ACT_TILES[:n]):
                            act.wait_ge(shift_ready, t.take("shift"))
                        last = normalise(R[:, b], tiles)
                        if not any(ACT_TILES[n + 1:]):
                            last.then_inc(z2_act, 1)
                if second:
                    drain("F2", ga[:], K1)
                    drain("F1", gb[:], K1)
                    drain("F2", ga[0:H, :], H)
                    drain("F1", gb[0:H, :], H)

            nodes(3, True, False)
            with t.loop(act, PAIRS // RING - 1, {"F0": 3 * RING, "F1": 5 * RING, "F2": 2 * RING, "shift": RING}):
                for b in range(RING):
                    nodes(b, True, True)
            for b in range(RING):
                nodes(b, b < RING - 1, True)

            with t.loop(act, EUNITS, {"F2": 4}) as i:
                for k in range(4):
                    if k == 0:
                        act.wait_ge(same_ready, 1)
                    drain("F2", state[:, bass.ds((4 * i + k) * COLS, COLS)], K1)

            for l in range(3):
                with t.loop(act, EUNITS, {"F0": 2 * (l > 0), "F1": 2 * (l < 2)}) as i:
                    for u in range(2):
                        c = 2 * i + u
                        if l:
                            drain("F0", state[:, bass.ds(c * COLS, COLS)], K1)
                        if l < 2:
                            drain("F1", state[:, bass.ds(SLOTS + c * COLS, COLS)], K1)

            act.wait_ge(done["F0"], t.at("F0", 0) + 1)
            act.wait_ge(done["F1"], t.at("F1", 0) + 1)

            def copy_states(q):
                nc.scalar.activation(ha[:], state[:, bass.ds(q * COLS, COLS)], ACT.Copy)
                nc.scalar.activation(hb[:], state[:, bass.ds(SLOTS + q * COLS, COLS)], ACT.Copy)\
                    .then_inc(state_copied, 1)

            def last_step(turn, u, a, b, more=True):
                q = 2 * turn + u
                if b:
                    drain("F0", state[:, bass.ds((q - 1) * COLS, COLS)], K1)
                    drain("F1", state[:, bass.ds(SLOTS + (q - 1) * COLS, COLS)], K1)
                    drain("F2", state[0:H, bass.ds((q - 1) * COLS, COLS)], H, order=True)
                if a:
                    drain("F2", ga[0:H, :], H, relu=False)
                    act.wait_ge(full["N1"], t.take("N1", 2))
                    if more:
                        copy_states(q + 1)
                    act.wait_ge(shift_ready, t.take("shift"))
                    normalise(R[:, u], LAST_ACT).then_inc(z2_act, 1)
                if b:
                    drain("F1", gb[0:H, :], H)

            copy_states(0)
            t.base["N1"] = N1_LAST
            last_step(0, 0, True, False)
            t.base["N1"] = N1_LAST - 1
            last_step(0, 1, True, True)
            last_step(1, 0, True, True)
            last_step(1, 1, True, True)
            with t.loop(act, EUNITS - 3, {"F0": 2, "F1": 4, "F2": 4, "N1": 4, "shift": 2}) as i:
                for u in range(2):
                    last_step(i + 2, u, True, True)
            last_step(EUNITS - 1, 0, True, True)
            last_step(EUNITS - 1, 1, True, True, more=False)
            last_step(EUNITS, 0, False, True)

        @block.vector
        def _(dve):
            t = Tally()
            for name in Nb:
                dve.sem_inc(done[name], 1)
            for u in range(2):
                dve.sem_inc(g_zero[u], 1)
            nc.vector.memset(rows_i[:, 0, :], 0)
            nc.vector.memset(rows_i[:, 1, :], BIG)
            nc.vector.memset(rows_i[:, 2, :], -1)
            nc.vector.memset(big[:], BIG).then_inc(consts_dve, 1)
            nc.vector.memset(WN[:], 0.0)
            nc.vector.memset(S[:], 0.0)
            nc.vector.memset(z1[:], 1.0)
            nc.vector.memset(z2[:], 1.0)
            nc.vector.memset(ga[:], 1.0)
            nc.vector.memset(gb[:], 1.0)
            nc.vector.memset(WS[:], 0.0)
            nc.vector.memset(same[:], 0.0).then_inc(consts_dve, 1)

            dve.wait_ge(consts_dve, 2)
            nc.vector.memset(WN[H:K1, H:K1], 1.0)
            nc.vector.memset(WS[H:K1, H:K1], 1.0).then_inc(consts_dve, 1)

            dve.wait_ge(done["F0"], 2)
            dve.wait_ge(loaded_b, 16 * 6)
            nc.vector.tensor_scalar(eps1[:], eps1[:], 1.0, None, ALU.add).then_inc(dve_prep, 1)
            dve.wait_ge(dve_prep, 1)
            nc.vector.tensor_scalar(W1S[0:H, :], W1S[0:H, :], eps1[0:H, :], None, ALU.mult).then_inc(weights_sb, 1)

            dve.wait_ge(loaded_rows, 16 * 6)
            nc.vector.tensor_copy(rows_f[:, 0, :], rows_i[:, 0, :])
            nc.vector.tensor_scalar(rows_f[:, 1, :], rows_i[:, 1, :], float(N_NODES - 1), None, ALU.min)
            nc.vector.tensor_tensor(cont[:], rows_i[:, 1, :], rows_i[:, 2, :], ALU.is_equal).then_inc(dve_prep, 1)
            dve.wait_ge(dve_prep, 2)
            nc.vector.tensor_scalar(cont[:], cont[:], float(BIG), None, ALU.mult).then_inc(dve_prep, 1)
            dve.wait_ge(dve_prep, 3)
            nc.vector.tensor_tensor(rows_f[:, 2, :], cont[:], rows_i[:, 1, :], ALU.add).then_inc(rows_ready, 1)
            dve.wait_ge(full["N0"], t.take("N0"))
            dve.wait_ge(consts_pool, 4)
            idx_t = Nb["N0"]
            nc.vector.tensor_copy(x_idx[:, 0:ETILES], idx_t[:, 0:ETILES]).then_inc(idx_ready, 1)
            nc.vector.tensor_copy(x_idx[:, ETILES:2 * ETILES], idx_t[:, ETILES:2 * ETILES]).then_inc(idx_ready, 1)
            nc.vector.tensor_copy(end_idx[:, :, 0], idx_t[:, 2 * ETILES:3 * ETILES]).then_inc(idx_ready, 1)
            dve.wait_ge(idx_ready, 3)
            dve.sem_inc(done["N0"], 1)
            dve.wait_ge(loaded_dst, 32)
            dst_all = state[:, SLOTS:SLOTS + N_EDGES].bitcast(i32)
            nc.vector.tensor_tensor(same[:, 1:N_EDGES], dst_all[:, 1:N_EDGES], dst_all[:, 0:N_EDGES - 1],
                                    ALU.is_equal).then_inc(same_ready, 1)

            def tick(last):
                last.then_inc(ln_tick, 1)
                dve.wait_ge(ln_tick, t.take("ln"))

            def statistics(rows, col):
                for k in range(UNIT):
                    last = nc.vector.bn_stats(st[:, col + k, :], rows[:, k, :])
                return last

            def moments(c):
                nc.vector.tensor_tensor(mean[:, c], st[:, c, 1], st[:, c, 4], ALU.add)
                nc.vector.tensor_tensor(diff[:, c], st[:, c, 1], st[:, c, 4], ALU.subtract)
                tick(nc.vector.scalar_tensor_tensor(out=var[:, c], in0=st[:, c, 2], scalar=H * LN_EPS,
                                                    in1=st[:, c, 5], op0=ALU.add, op1=ALU.add))
                nc.vector.tensor_scalar(mean[:, c], mean[:, c], 0.5, None, ALU.mult)
                tick(nc.vector.scalar_tensor_tensor(out=diff[:, c], in0=diff[:, c], scalar=-0.125, in1=diff[:, c],
                                                    op0=ALU.mult, op1=ALU.mult))
                tick(nc.vector.scalar_tensor_tensor(out=var[:, c], in0=var[:, c], scalar=-0.5 / H,
                                                    in1=diff[:, c], op0=ALU.mult, op1=ALU.add))
                tick(nc.vector.tensor_scalar(rstd[:, c].bitcast(i32), var[:, c].bitcast(i32), -0.5, RSQRT_MAGIC,
                                             ALU.mult, ALU.add))
                tick(nc.vector.scalar_tensor_tensor(out=diff[:, c], in0=var[:, c], scalar=3.0 * RSQRT_K,
                                                    in1=rstd[:, c], op0=ALU.mult, op1=ALU.mult))
                tick(nc.vector.tensor_tensor(diff[:, c], diff[:, c], rstd[:, c], ALU.mult))
                tick(nc.vector.scalar_tensor_tensor(out=rstd[:, c], in0=diff[:, c], scalar=1.5 * RSQRT_C,
                                                    in1=rstd[:, c], op0=ALU.add, op1=ALU.mult))
                tick(nc.vector.scalar_tensor_tensor(out=diff[:, c], in0=var[:, c], scalar=1.0 / 2.25,
                                                    in1=rstd[:, c], op0=ALU.mult, op1=ALU.mult))
                tick(nc.vector.tensor_tensor(diff[:, c], diff[:, c], rstd[:, c], ALU.mult))
                tick(nc.vector.scalar_tensor_tensor(out=diff[:, c], in0=diff[:, c], scalar=5.0 / 3.0,
                                                    in1=diff[:, c], op0=ALU.add, op1=ALU.mult))
                tick(nc.vector.scalar_tensor_tensor(out=rstd[:, c], in0=diff[:, c], scalar=1.25,
                                                    in1=rstd[:, c], op0=ALU.add, op1=ALU.mult))

            def normalise(rows, z, col, tiles=range(UNIT)):
                for k in tiles:
                    last = nc.vector.tensor_scalar(z[:, k, 0:H], rows[:, k, :], mean[:, col + k:col + k + 1],
                                                   rstd[:, col + k:col + k + 1], ALU.subtract, ALU.mult)
                return last

            def layernorm(rows, z):
                tick(statistics(rows, UNIT))
                moments(slice(UNIT, 2 * UNIT))
                return normalise(rows, z, UNIT)

            def add_rows(name, to, rows):
                dve.wait_ge(full[name], t.take(name))
                nc.vector.tensor_tensor(to, rows, Nb[name][:, 0:HALF * H].rearrange("p (t f) -> p t f", f=H),
                                        ALU.add).then_inc(done[name], 1)

            lo, hi = slice(0, HALF), slice(HALF, UNIT)

            def nodes(i, k, first=True, second=True, ahead=True):
                t.take("F1", 3 * first + 2 * second)
                mine, before = R[:, (k + 2) % RING], R[:, (k + 1) % RING]
                if first:
                    add_rows("N0", mine[:, lo], mine[:, lo])
                    add_rows("N1", mine[:, hi], mine[:, hi])
                    dve.wait_ge(done["N1"], t.at("N1", 0) + 1)
                    last = statistics(mine, 0)
                    if ahead:
                        dve.wait_ge(x_in[k], 16 * (i + 2))
                        last = statistics(R[:, k], UNIT)
                    tick(last)
                    if second:
                        dve.wait_ge(z2_act, t.take("z2_act"))
                    moments(slice(0, 2 * UNIT if ahead else UNIT))
                    nc.vector.scalar_tensor_tensor(out=shift[:], in0=mean[:, 0:UNIT], scalar=-1.0,
                                                   in1=rstd[:, 0:UNIT], op0=ALU.mult, op1=ALU.mult)\
                        .then_inc(shift_ready, 1)
                if second:
                    add_rows("N0", before[:, lo], before[:, lo])
                    add_rows("N1", before[:, hi], before[:, hi])
                if first:
                    if second:
                        dve.wait_ge(full["F1"], t.at("F1", -1))
                    normalise(mine, z2, 0, OWN_TILES).then_inc(z_full["z2"], 1)
                if ahead:
                    dve.wait_ge(full["F1"], t.at("F1"))
                    normalise(R[:, k], z1, UNIT).then_inc(z_full["z1"], 1)

            for q in range(2):
                dve.wait_ge(x_in[q], 16)
                if q:
                    dve.wait_ge(full["F1"], t.at("F1"))
                layernorm(R[:, q], z1).then_inc(z_full["z1"], 1)
            nodes(-1, 2, second=False)
            nodes(-1, 3)
            turns = PAIRS // RING - 1
            with t.loop(dve, turns, {"F1": 5 * RING, "N0": 2 * RING, "N1": 2 * RING, "ln": RING * LN_TICKS,
                                     "z2_act": RING}) as i:
                for k in range(RING):
                    nodes(i, k)
            nodes(turns, 0, ahead=False)
            nodes(turns, 1, ahead=False)
            nodes(turns, 2, first=False, ahead=False)
            t.take("F2", 2 * PAIRS)

            with t.loop(dve, EUNITS, {"ln": 2 * LN_TICKS, "rows": 1, "F2": 4}):
                for u in range(2):
                    dve.wait_ge(xg_in[u], 16 * UNIT * t.at("rows"))
                    dve.wait_ge(full["F2"], t.at("F2", 0))
                    t.take("F2", 2)
                    layernorm(xg[:, u], z1).then_inc(zg_full, 1)
                t.take("rows")

            def scan(c, u, data):
                if not (isinstance(c, int) and c == 0):
                    dve.wait_ge(scanned, t.at("scan", 0))
                nc.vector.tensor_tensor_scan(S[:, u], same[:, bass.ds(c * COLS, COLS)], data,
                                             S[:, 1 - u, COLS - 1:COLS], ALU.mult, ALU.add)\
                    .then_inc(scanned, 1)
                t.take("scan")

            dve.wait_ge(same_ready, 1)
            dve.wait_ge(done["F2"], t.at("F2", 0) + 1)

            def messages(l, c, u, first):
                if l:
                    dve.wait_ge(done["F0"], t.take("F0") + 1)
                scan(c, u, state[:, bass.ds(c * COLS, COLS)])
                if l:
                    nc.vector.memset(G[:, u], 0.0).then_inc(g_zero[u], 1)
                dve.wait_ge(full["N0"], t.take("N0"))
                sums = Nb["N0"][:, 0:HALF * K1].rearrange("p (t f) -> p t f", f=K1)
                if l == 0:
                    nc.vector.reciprocal(rdeg[:, bass.ds(c * HALF, HALF)], sums[:, :, H]).then_inc(deg_done, 1)
                    dve.wait_ge(deg_done, t.take("deg"))
                if not first:
                    dve.wait_ge(t_out[u], 16 * t.at("t_out", 0))
                    dve.wait_ge(full["F1"], t.at("F1", 0) - 1)
                t.take("F1", int(l < 2))
                nc.vector.tensor_tensor(T[:, u], sums[:, :, 0:H],
                                        rdeg[:, bass.ds(c * HALF, HALF)].unsqueeze(2).broadcast_to([P, HALF, H]),
                                        ALU.mult).then_inc(t_full, 1)
                dve.wait_ge(t_full, t.take("T"))
                dve.sem_inc(done["N0"], 1)

            t.take("F0")
            t.take("F0", 3 * PAIRS)
            for l in range(3):
                per = {"scan": 2, "N0": 2, "T": 2, "t_out": 1, "deg": 2 * (l == 0), "F1": 2 * (l < 2),
                       "F0": 2 * (l > 0), "g": 0}
                start = 0
                if l == 0:
                    for u in range(2):
                        messages(l, u, u, True)
                    t.take("t_out")
                    start = 1
                with t.loop(dve, EUNITS - start, per) as i:
                    for u in range(2):
                        messages(l, 2 * i + 2 * start + u, u, False)
                    t.take("t_out")

            dve.wait_ge(y_out[2], 16 * (PAIRS // RING))
            dve.wait_ge(y_out[3], 16 * (PAIRS // RING))

            def last_step(turn, u, a, b, c, reused=True):
                if a:
                    dve.wait_ge(e_in[u], 16 * 4 * (turn + 1))
                    add_rows("N0", R[:, u, lo], xg[:, u, lo])
                if c:
                    if reused:
                        dve.wait_ge(yo[u], 16 * HALF * (turn - 1))
                    add_rows("N1", R[:, 2 + u, lo], R[:, u, hi])
                if a:
                    add_rows("N1", R[:, u, hi], xg[:, u, hi])
                    nc.vector.memset(G[:, u], 0.0).then_inc(g_zero[u], 1)
                    dve.wait_ge(done["N1"], t.at("N1", 0) + 1)
                    tick(statistics(R[:, u], 0))
                    dve.wait_ge(z2_act, t.take("z2_act"))
                    moments(slice(0, UNIT))
                    nc.vector.scalar_tensor_tensor(out=shift[:], in0=mean[:, 0:UNIT], scalar=-1.0,
                                                   in1=rstd[:, 0:UNIT], op0=ALU.mult, op1=ALU.mult)\
                        .then_inc(shift_ready, 1)
                if b:
                    q = 2 * turn + u - 1
                    dve.wait_ge(done["F2"], t.take("F2", 1) + 1)
                    dve.wait_ge(scanned, t.at("scan", 0))
                    nc.vector.tensor_tensor_scan(S[0:H, 1 - u], same[0:H, bass.ds(q * COLS, COLS)],
                                                 state[0:H, bass.ds(q * COLS, COLS)], S[0:H, u, COLS - 1:COLS],
                                                 ALU.mult, ALU.add).then_inc(scanned, 1)
                    dve.wait_ge(scanned, t.take("scan"))
                    dve.wait_ge(done["F1"], t.take("F1", 2) + 1)
                    nc.vector.scalar_tensor_tensor(out=gb[0:H, :], in0=state[0:H, bass.ds(SLOTS + q * COLS, COLS)],
                                                   scalar=eps1[0:H, :], in1=S[0:H, 1 - u], op0=ALU.mult,
                                                   op1=ALU.add).then_inc(h_mixed, 1)
                if a:
                    t.take("F2", 1)
                    own = [k for k in range(UNIT) if k not in LAST_ACT]
                    normalise(R[:, u], z2, 0, own).then_inc(z_full["z2"], 1)

            for turn in range(2):
                for u in range(2):
                    last_step(turn, u, True, turn + u > 0, turn > 0, reused=False)
            with t.loop(dve, EUNITS - 2, {"N0": 2, "N1": 4, "ln": 2 * LN_TICKS, "F2": 4, "F1": 4, "scan": 2,
                                          "z2_act": 2}) as i:
                for u in range(2):
                    last_step(i + 2, u, True, True, True)
            last_step(EUNITS, 0, False, True, True)
            last_step(EUNITS, 1, False, False, True)


_INS = ["x", "src", "dst", "edge_attr_96", "L0_gnn_W_self", "L0_gnn_W_neigh", "L0_gnn_b", "L1_gnn_W_edge",
        "L1_gnn_b_edge", "L1_gnn_eps", "L1_gnn_W1", "L1_gnn_b1", "L1_gnn_W2", "L1_gnn_b2"]


def kernel(**inputs):
    import concourse.bacc as bacc
    from concourse.bass_utils import run_bass_kernel_spmd

    nc = bacc.Bacc("TRN2", target_bir_lowering=False, num_devices=1)
    arrays, args = {}, []
    for name in _INS:
        a = np.ascontiguousarray(inputs[name])
        if a.ndim == 0:
            a = a.reshape(1)
        arrays["in_" + name] = a
        args.append(nc.dram_tensor("in_" + name, a.shape, mybir.dt.from_np(a.dtype), kind="ExternalInput").ap())
    out = nc.dram_tensor("out", (N_NODES, H), f32, kind="ExternalOutput").ap()
    (x, src, dst, edge_attr, w_self, w_neigh, b, w_edge, b_edge, eps, w1, b1, w2, b2) = args
    build(nc, x, src, dst, edge_attr, w_self, w_neigh, b, w_edge, b_edge, eps, w1, b1, w2, b2, out)
    return run_bass_kernel_spmd(nc, [arrays], core_ids=[0]).results[0]["out"]
```

```python
from collections import Counter
from contextlib import ExitStack, contextmanager

import numpy as np

import concourse.bass as bass
from concourse import mybir

N_NODES = 50000
N_EDGES = 12500
H = 96
LN_EPS = 1e-5

P = 128
RING = 4
ACT_TILES = ((), (), (0, 1), (2, 3), (4, 5), (6, 7))
OWN_TILES = (8, 9)
LAST_ACT = range(5)
HALF = 5
UNIT = 2 * HALF
COLS = HALF * P
K1 = H + 1
PAIRS = -(-N_NODES // (UNIT * P))
ROWS = N_NODES // (P * UNIT) * UNIT
SLOTS = -(-N_EDGES // (UNIT * P)) * UNIT * P
ETILES = SLOTS // P
EUNITS = ETILES // UNIT
CHUNKS = 2 * EUNITS
FULL_ROWS = N_EDGES // P
REST = N_EDGES - FULL_ROWS * P
MAP_ROWS = 80
BIG = 1 << 17

f32, bf16, i32 = mybir.dt.float32, mybir.dt.bfloat16, mybir.dt.int32
ALU = mybir.AluOpType
ACT = mybir.ActivationFunctionType


class Tally:

    def __init__(self):
        self.base, self.now, self.per, self.i = Counter(), Counter(), {}, None

    def at(self, name, k=1):
        fixed = self.base[name] + self.now[name] + k
        if self.i is None or not self.per.get(name):
            return fixed
        return self.i * self.per[name] + fixed

    def take(self, name, n=1):
        value = self.at(name)
        self.now[name] += n
        return value

    @contextmanager
    def loop(self, engine, times, per):
        self.base.update(self.now)
        self.now.clear()
        with engine.Fori(0, times) as i:
            self.i, self.per = i, per
            yield i
            for name, n in self.now.items():
                assert n == per.get(name, 0), (name, n, per.get(name))
        self.i, self.per = None, {}
        self.now.clear()
        for name, n in per.items():
            self.base[name] += n * times


LN_TICKS = 12
RSQRT_MAGIC = float(0x5F1FFFF9 - (1 << 22) - (1 << 30))
RSQRT_K, RSQRT_C = 0.703952253, 0.703952253 * 2.38924456
N1_LAST = 2 * PAIRS
F2_LAST = 2 * PAIRS
AFTER_0, WITH_1, WITH_2 = 1, 8, 5
LATE = PAIRS - (AFTER_0 + WITH_1 + 1 + WITH_2 + 1)
IN_1, IN_2 = LATE + AFTER_0, LATE + AFTER_0 + WITH_1 + 1
SIDES = 2 * EUNITS


def build(nc, x, src, dst, edge_attr, w_self, w_neigh, b_self, w_edge, b_edge, eps, w1, b1, w2, b2, out):
    slot_of_node = nc.dram_tensor("slot_of_node", (N_NODES, 1), i32, kind="Internal").ap()
    x_slots = nc.dram_tensor("x_slots", (2 * EUNITS, P, UNIT * H), f32, kind="Internal").ap()
    table = [nc.dram_tensor(f"neigh_table{l}", (SLOTS, H), f32, kind="Internal").ap() for l in range(3)]
    edge_rows = nc.dram_tensor("edge_rows", (SLOTS, H), f32, kind="Internal").ap()
    cont_rows = nc.dram_tensor("cont_rows", (SLOTS,), bf16, kind="Internal").ap()

    with ExitStack() as ctx:
        def sb(name, shape, dt=f32):
            return ctx.enter_context(nc.sbuf_tensor(name, shape, dt))

        def sem(name):
            return ctx.enter_context(nc.semaphore(name))

        ident = sb("ident", [P, P])
        w_raw = sb("w_raw", [H, 5, H])
        WS = sb("WS", [K1, K1])
        WN = sb("WN", [K1, K1])
        WE = sb("WE", [K1, H])
        W1 = sb("W1", [K1, H])
        W1S = sb("W1S", [K1, H])
        W2 = sb("W2", [K1, H])
        eps1 = sb("eps1", [P, 1])
        rows_i = sb("rows_i", [ETILES, 3, P], i32)
        rows_f = sb("rows_f", [ETILES, 3, P])
        cont = sb("cont", [ETILES, P])
        cont_b = sb("cont_b", [ETILES, P], bf16)
        x_idx = sb("x_idx", [P, 2 * ETILES], i32)
        end_idx = sb("end_idx", [P, ETILES, 2], i32)
        q_idx = sb("q_idx", [P, ETILES], i32)
        big = sb("big", [MAP_ROWS, N_NODES // MAP_ROWS], i32)
        iring = sb("iring", [P, 2, UNIT], i32)
        ering = sb("ering", [P, 2, UNIT, 2], i32)
        qring = sb("qring", [P, 2, UNIT], i32)
        R = sb("R", [P, RING, UNIT, H])
        z1 = sb("z1", [P, UNIT, K1])
        z2 = sb("z2", [P, UNIT, K1])
        zx = sb("zx", [P, UNIT, K1])
        ha = sb("ha", [K1, COLS])
        hb = sb("hb", [K1, COLS])
        ga = sb("ga", [K1, COLS])
        gb = sb("gb", [K1, COLS])
        state = sb("state", [K1, 2 * SLOTS])
        same = sb("same", [K1, SLOTS], bf16)
        xg = sb("xg", [P, 2, UNIT, H])
        G = sb("G", [P, 2, HALF, H])
        T = sb("T", [P, 2, HALF, H])
        S = sb("S", [K1, 2, COLS])
        rdeg = sb("rdeg", [P, ETILES])
        er = sb("er", [P, 2, HALF, H])
        st = sb("st", [P, 3 * UNIT, 6])
        mean = sb("mean", [P, 3 * UNIT])
        diff = sb("diff", [P, 3 * UNIT])
        var = sb("var", [P, 3 * UNIT])
        rstd = sb("rstd", [P, 3 * UNIT])
        shift = sb("shift", [P, UNIT])

        F = {f"F{k}": ctx.enter_context(nc.psum_tensor(f"F{k}", [P, 1024], f32)) for k in range(3)}
        Nb = {f"N{k}": ctx.enter_context(nc.psum_tensor(f"N{k}", [P, 512], f32)) for k in range(2)}

        full = {k: sem(f"{k}_full") for k in (*F, *Nb)}
        done = {k: sem(f"{k}_done") for k in (*F, *Nb)}
        z_full = {k: sem(f"{k}_full") for k in ("z1", "z2")}
        z2_act = sem("z2_act")
        shift_ready = sem("shift_ready")
        ln_tick = sem("ln_tick")
        x_in = [sem(f"x_in{b}") for b in range(RING)]
        y_out = [sem(f"y_out{b}") for b in range(RING)]
        xg_in = [sem(f"xg_in{u}") for u in range(2)]
        xg_out = [sem(f"xg_out{u}") for u in range(2)]
        zg_full = sem("zg_full")
        idx_copied = sem("idx_copied")
        map_in = [sem(f"map_in{u}") for u in range(2)]
        q_in = [sem(f"q_in{u}") for u in range(2)]
        q_copied = sem("q_copied")
        pool_order = sem("pool_order")
        act_order = sem("act_order")
        g_zero = [sem(f"g_zero{u}") for u in range(2)]
        g_in = [sem(f"g_in{u}") for u in range(2)]
        scanned = sem("scanned")
        deg_done = sem("deg_done")
        t_full = sem("t_full")
        t_out = [sem(f"t_out{u}") for u in range(2)]
        loaded_w = sem("loaded_w")
        loaded_b = sem("loaded_b")
        loaded_rows = sem("loaded_rows")
        cont_ready = sem("cont_ready")
        cont_out = sem("cont_out")
        consts_pool = sem("consts_pool")
        consts_dve = sem("consts_dve")
        weights_t = sem("weights_t")
        weights_sb = sem("weights_sb")
        rows_ready = sem("rows_ready")
        rows_t = sem("rows_t")
        idx_ready = sem("idx_ready")
        same_ready = sem("same_ready")
        dve_prep = sem("dve_prep")
        map_cleared = sem("map_cleared")
        edges_copied = sem("edges_copied")
        e_in = [sem(f"e_in{u}") for u in range(2)]
        state_copied = sem("state_copied")
        h_mixed = sem("h_mixed")
        yo = [sem(f"yo{u}") for u in range(2)]

        def node_rows(t, pair):
            own = t[0:P * ROWS, :].rearrange("(p r) f -> p r f", p=P)
            return own[:, bass.ds(pair * UNIT, UNIT), :]

        def last_rows(t):
            return t[N_NODES - P * UNIT:N_NODES, :].rearrange("(p r) f -> p r f", p=P)

        def slot_rows(t, chunk):
            return t[bass.ds(chunk * COLS, COLS), :].rearrange("(t p) f -> p t f", p=P)

        block = ctx.enter_context(nc.Block())

        @block.sync
        def _(sp):
            t = Tally()
            for n, w in enumerate((w_self, w_neigh, w_edge, w1, w2)):
                sp.dma_start(w_raw[:, n, :], w).then_inc(loaded_w, 16)
            sp.dma_start(R[:, 0], node_rows(x, 0)).then_inc(x_in[0], 16)
            sp.wait_ge(consts_dve, 1)
            cut = FULL_ROWS * P
            for k, (v, off) in enumerate(((src, 0), (dst, 0), (dst, 1))):
                sp.dma_start(rows_i[0:FULL_ROWS, k, :], v[off:off + cut].rearrange("(t p) -> t p", p=P))\
                    .then_inc(loaded_rows, 16)
                sp.dma_start(rows_i[FULL_ROWS:FULL_ROWS + 1, k, 0:REST - off],
                             v[cut + off:N_EDGES].rearrange("(t p) -> t p", t=1)).then_inc(loaded_rows, 16)
            sp.dma_start(slot_of_node.rearrange("(p r) a -> p (r a)", p=MAP_ROWS), big[:])\
                .then_inc(map_cleared, 16)
            for q in range(1, RING):
                sp.dma_start(R[:, q], node_rows(x, q)).then_inc(x_in[q], 16)
            sp.wait_ge(consts_dve, 3)
            for m, b in ((WS, b_self), (WE, b_edge), (W1, b1), (W1S, b1), (W2, b2)):
                sp.dma_start(m[H:K1, 0:H], b.rearrange("(a f) -> a f", a=1)).then_inc(loaded_b, 16)
            sp.dma_start(eps1[:], eps.rearrange("(a f) -> a f", a=1).broadcast_to([P, 1])).then_inc(loaded_b, 16)
            sp.dma_start(edge_rows[0:N_EDGES, :].rearrange("(r s) f -> r (s f)", r=4 * 25),
                         edge_attr.rearrange("(r s) f -> r (s f)", r=4 * 25)).then_inc(edges_copied, 16)
            sp.wait_ge(consts_pool, 2)
            pad = SLOTS - N_EDGES
            sp.dma_start(edge_rows[N_EDGES:SLOTS, :].rearrange("(r s) f -> r s f", s=3),
                         G[0:pad // 3, 0, 0:3, :]).then_inc(edges_copied, 16)

            sp.wait_ge(cont_ready, 1)
            sp.dma_start(cont_rows.rearrange("(t p) -> t p", p=P), cont_b[:]).then_inc(cont_out, 16)
            sp.wait_ge(cont_out, 16)
            sp.dma_start(same[:, 1:SLOTS], cont_rows[0:SLOTS - 1].rearrange("(a e) -> a e", a=1)
                         .broadcast_to([K1, SLOTS - 1])).then_inc(same_ready, 16)

            def nodes(i, k, load=True, sage=True, last=False, slots=False):
                if load:
                    sp.wait_ge(y_out[k], 16 * (i + 1))
                    rows = last_rows(x) if last else node_rows(x, 4 * i + 4 + k)
                    sp.dma_start(R[:, k], rows).then_inc(x_in[k], 16)
                t.take("N1", int(sage))
                sp.wait_ge(done["N1"], t.take("N1") + 1)
                b = (k + 1) % RING
                if last and not load:
                    for j in range(RING):
                        sp.wait_ge(y_out[j], 16 * (PAIRS // RING - (j == b)))
                rows = last_rows(out) if last and not load else node_rows(out, 4 * i + 1 + k)
                sp.dma_start(rows, R[:, b]).then_inc(y_out[b], 16)
                if slots:
                    u = k % 2
                    sp.wait_ge(xg_in[u], 16 * UNIT * (2 * i + k // 2 + 1))
                    sp.dma_start(x_slots[bass.ds(4 * i + k, 1), :, :].rearrange("a p c -> (a p) c"),
                                 xg[:, u].rearrange("p t f -> p (t f)")).then_inc(xg_out[u], 16)

            t.take("N1")
            nodes(-1, 3, load=False)
            with t.loop(sp, SIDES // RING, {"N1": 8}) as i:
                for k in range(RING):
                    nodes(i, k, slots=True)
            def step(q, **more):
                nodes((q - 2) // RING, (q - 2) % RING, **more)

            for q in range(SIDES + 2, LATE):
                step(q)

            def store(l, chunk, u):
                sp.wait_ge(t_full, t.take("T"))
                sp.dma_start(slot_rows(table[l], chunk), T[:, u]).then_inc(t_out[u], 16)

            def turn_stores(l, turn):
                store(l, 2 * turn - 1, 1)
                store(l, 2 * turn, 0)

            store(0, 0, 0)
            with t.loop(sp, EUNITS - 1, {"T": 2}) as i:
                turn_stores(0, i + 1)
            store(0, CHUNKS - 1, 1)
            for q in range(LATE, IN_1):
                step(q)
            store(1, 0, 0)
            with t.loop(sp, WITH_1 // RING, {"T": 2 * RING, "N1": 2 * RING}) as i:
                for k in range(RING):
                    turn_stores(1, 4 * i + 1 + k)
                    nodes(i + (IN_1 - 2 + k) // RING, (IN_1 - 2 + k) % RING)
            turn_stores(1, EUNITS - 1)
            store(1, CHUNKS - 1, 1)
            step(IN_2 - 1)
            store(2, 0, 0)
            for turn in range(1, 1 + WITH_2):
                turn_stores(2, turn)
                q = IN_2 + turn - 1
                step(q, load=q < PAIRS - 2, last=q == PAIRS - 3)
            with t.loop(sp, EUNITS - 1 - WITH_2, {"T": 2}) as i:
                turn_stores(2, i + 1 + WITH_2)
            store(2, CHUNKS - 1, 1)
            sp.wait_ge(t_out[0], 16 * 3 * EUNITS)
            sp.wait_ge(t_out[1], 16 * 3 * EUNITS)
            sp.wait_ge(xg_out[0], 16 * EUNITS)
            sp.wait_ge(xg_out[1], 16 * EUNITS)
            sp.wait_ge(edges_copied, 32)

            def last_loads(turn, u, n1=None):
                if n1 is not None:
                    sp.wait_ge(done["N1"], n1)
                for k, j in ((0, turn), (1, turn + EUNITS)):
                    sp.dma_start(xg[:, u, k * HALF:(k + 1) * HALF, :].rearrange("p t f -> p (t f)"),
                                 x_slots[bass.ds(j, 1), :, u * HALF * H:(u + 1) * HALF * H]
                                 .rearrange("a p c -> (a p) c")).then_inc(e_in[u], 16)
                sp.dma_start(T[:, u], slot_rows(table[2], 2 * turn + u)).then_inc(e_in[u], 16)
                if n1 is not None:
                    sp.wait_ge(full["F2"], F2_LAST + 1 + 2 * (2 * turn + u - 2))
                sp.dma_start(er[:, u], slot_rows(edge_rows, 2 * turn + u)).then_inc(e_in[u], 16)

            last_loads(0, 0)
            last_loads(0, 1)
            step(PAIRS - 1, load=False)
            step(PAIRS, load=False, sage=False, last=True)
            last_loads(1, 0, N1_LAST + 2)
            last_loads(1, 1, N1_LAST + 3)
            with t.loop(sp, EUNITS - 2, {}) as i:
                for u in range(2):
                    last_loads(i + 2, u, N1_LAST + 2 * (2 * i + 2 + u))
            sp.wait_ge(yo[0], 16 * HALF * EUNITS)
            sp.wait_ge(yo[1], 16 * HALF * EUNITS)

        @block.gpsimd
        def _(pool):
            t = Tally()
            pool.memset(ident[:], 0.0).then_inc(consts_pool, 1)
            pool.memset(G[:], 0.0).then_inc(consts_pool, 1)
            pool.wait_ge(consts_pool, 2)
            pool.affine_select(out=ident[:], in_=ident[:], compare_op=ALU.not_equal, fill=1.0, base=0,
                               pattern=[[-1, P]], channel_multiplier=1).then_inc(consts_pool, 1)
            pool.iota(end_idx[:, :, 1], pattern=[[P, ETILES]], base=0, channel_multiplier=1)\
                .then_inc(consts_pool, 1)
            pool.wait_ge(consts_pool, 4)

            def order():
                pool.sem_inc(pool_order, 1)

            def copy_indices(to, of):
                pool.tensor_copy(to, of).then_inc(idx_copied, 1)
                pool.wait_ge(idx_copied, t.take("copy"))
                order()

            def map_chunk(chunk, u, uses):
                if uses is not None:
                    pool.wait_ge(map_in[u], 16 * HALF * uses)
                    order()
                copy_indices(ering[:, u, 0:HALF], end_idx[:, bass.ds(chunk * HALF, HALF), :])
                for k in range(HALF):
                    pool.indirect_dma_start(
                        out=slot_of_node, out_offset=bass.IndirectOffsetOnAxis(ap=ering[:, u, k, 0:1], axis=0),
                        in_=ering[:, u, k, 1:2], in_offset=None, bounds_check=N_NODES - 1,
                        oob_is_err=False).then_inc(map_in[u], 16)

            def map_lookup(unit, u):
                copy_indices(iring[:, u], x_idx[:, bass.ds(unit * UNIT, UNIT)])
                for k in range(UNIT):
                    pool.indirect_dma_start(
                        out=qring[:, u, k:k + 1], out_offset=None, in_=slot_of_node,
                        in_offset=bass.IndirectOffsetOnAxis(ap=iring[:, u, k:k + 1], axis=0),
                        bounds_check=N_NODES - 1, oob_is_err=False).then_inc(q_in[u], 16)

            def rows_unit(unit, u, first):
                if not first:
                    pool.wait_ge(xg_out[u], 16 * t.at("rows", 0))
                    order()
                    pool.wait_ge(zg_full, t.at("zg") - 2)
                    order()
                t.take("zg")
                copy_indices(iring[:, u], x_idx[:, bass.ds(unit * UNIT, UNIT)])
                for k in range(UNIT):
                    pool.indirect_dma_start(
                        out=xg[:, u, k, :], out_offset=None, in_=x,
                        in_offset=bass.IndirectOffsetOnAxis(ap=iring[:, u, k:k + 1], axis=0),
                        bounds_check=N_NODES - 1, oob_is_err=False).then_inc(xg_in[u], 16)

            pool.wait_ge(idx_ready, 3)
            rows_unit(0, 0, True)
            rows_unit(1, 1, True)
            pool.wait_ge(map_cleared, 16)
            for chunk in range(4):
                map_chunk(chunk, chunk % 2, 1 if chunk > 1 else None)
            t.take("rows")
            with t.loop(pool, EUNITS - 2, {"copy": 4, "rows": 1, "zg": 2}) as i:
                for u in range(2):
                    rows_unit(2 * i + (2 + u), u, False)
                    map_chunk(2 * i + (4 + u), u, i + 2)
                t.take("rows")
            for u in range(2):
                rows_unit(SIDES - 2 + u, u, False)
            t.take("rows")
            for u in range(2):
                pool.wait_ge(map_in[u], 16 * HALF * EUNITS)
                pool.wait_ge(xg_in[u], 16 * UNIT * EUNITS)
            with t.loop(pool, EUNITS // 2, {"copy": 2, "q": 1}) as i:
                for u in range(2):
                    map_lookup(2 * i + u, u)
                for u in range(2):
                    pool.wait_ge(q_in[u], 16 * UNIT * t.at("q"))
                    order()
                    pool.tensor_copy(q_idx[:, bass.ds((2 * i + u) * UNIT, UNIT)], qring[:, u])\
                        .then_inc(q_copied, 1)
                t.take("q")

            def neighbours(l, c, u, use):
                pool.wait_ge(g_zero[u], use)
                order()
                copy_indices(iring[:, u, 0:HALF], q_idx[:, bass.ds(c * HALF, HALF)])
                for k in range(HALF):
                    pool.indirect_dma_start(
                        out=G[:, u, k, :], out_offset=None, in_=table[l],
                        in_offset=bass.IndirectOffsetOnAxis(ap=iring[:, u, k:k + 1], axis=0),
                        bounds_check=SLOTS - 1, oob_is_err=False).then_inc(g_in[u], 16)

            pool.wait_ge(q_copied, EUNITS)
            pool.wait_ge(edges_copied, 32)
            for l in range(2):
                for u in range(2):
                    pool.wait_ge(t_out[u], 16 * EUNITS * (l + 1))
                with t.loop(pool, EUNITS, {"copy": 2, "g": 1}) as i:
                    for u in range(2):
                        neighbours(l, 2 * i + u, u, t.at("g"))
                    t.take("g")
            for u in range(2):
                pool.wait_ge(t_out[u], 16 * EUNITS * 3)


            def scatter(c, b, use, y=4):
                u = b % 2
                if use is not None:
                    pool.wait_ge(yo[u], 16 * HALF * use)
                    order()
                copy_indices(ering[:, u, 0:HALF], end_idx[:, bass.ds(c * HALF, HALF), :])
                pool.wait_ge(done["N1"], N1_LAST + 1 + 2 * c + y)
                order()
                for k in range(HALF):
                    pool.indirect_dma_start(
                        out=out, out_offset=bass.IndirectOffsetOnAxis(ap=ering[:, u, k, 0:1], axis=0),
                        in_=R[:, b, HALF + k, :], in_offset=None, bounds_check=N_NODES - 1,
                        oob_is_err=False).then_inc(yo[u], 16)

            def gather(c, use):
                neighbours(2, c, use[1], 2 * EUNITS + use[0] + 1)

            for c in range(3):
                gather(c, (c // 2, c % 2))
            for b in range(RING):
                pool.wait_ge(y_out[b], 16 * (PAIRS // RING))
            for c in range(RING):
                gather(c + 3, ((c + 3) // 2, (c + 3) % 2))
                scatter(c, c, c // 2 if c > 1 else None)
            with t.loop(pool, CHUNKS // RING - 2, {"copy": 2 * RING}) as i:
                for b in range(RING):
                    gather(4 * i + (RING + b + 3), (2 * i + (RING + b + 3) // 2, (b + 3) % 2))
                    scatter(4 * i + (RING + b), b, 2 * i + (RING + b) // 2)
            gather(CHUNKS - 1, ((CHUNKS - 1) // 2, 1))
            for b in range(RING):
                c = CHUNKS - RING + b
                scatter(c, b, c // 2, y=(4, 4, 3, 2)[b])

        @block.tensor
        def _(pe):
            t = Tally()

            def claim(name):
                pe.wait_ge(done[name], t.at(name))

            def fill(name, last):
                last.then_inc(full[name], 1)
                t.take(name)

            def transposes(name, z):
                for k in range(HALF):
                    last = nc.tensor.transpose(F[name][0:z.shape[2], k * P:(k + 1) * P], z[:, k, :], ident[:])
                fill(name, last)

            def wide(name, w, h, rows, more=()):
                for lo, n in ((0, 512), (512, COLS - 512)):
                    tiles = [k for k in range(HALF) if lo <= k * P < lo + n] if more else []
                    last = nc.tensor.matmul(F[name][0:rows, lo:lo + n], w, h[:, lo:lo + n] if not callable(h)
                                            else h(lo, n), start=True, stop=True)
                    for k in tiles:
                        last = nc.tensor.matmul(F[name][0:H, k * P:(k + 1) * P], more[k], ident[:],
                                                start=False, stop=True, skip_group_check=True)
                fill(name, last)

            def tall(name, h, w, width, rows=None):
                if rows is not None:
                    nc.tensor.matmul(Nb[name][:, 0:HALF * width], ident[:], rows.rearrange("p t f -> p (t f)"),
                                     start=True, stop=True)
                for k in range(HALF):
                    last = nc.tensor.matmul(Nb[name][:, k * width:(k + 1) * width], h[:, k * P:(k + 1) * P], w,
                                            start=rows is None, stop=True, skip_group_check=rows is not None)
                fill(name, last)

            pe.wait_ge(consts_pool, 3)
            pe.wait_ge(loaded_w, 16 * 5)
            claim("F0")
            for n in range(5):
                last = nc.tensor.transpose(F["F0"][0:H, n * H:(n + 1) * H], w_raw[:, n, :],
                                           ident[0:H, 0:H])
            fill("F0", last)
            pe.wait_ge(rows_ready, 1)
            claim("N0")
            for k in range(3):
                last = nc.tensor.transpose(Nb["N0"][:, k * ETILES:(k + 1) * ETILES], rows_f[:, k, :],
                                           ident[0:ETILES, 0:ETILES])
            fill("N0", last)
            pe.wait_ge(weights_sb, 1)
            pe.wait_ge(loaded_b, 16 * 6)
            pe.wait_ge(consts_dve, 3)

            def nodes(first, second, slots=False):
                if first:
                    pe.wait_ge(z_full["z1"], t.take("z1"))
                    claim("F0")
                    transposes("F0", z1[:, 0:HALF, :])
                    claim("F1")
                    transposes("F1", z1[:, HALF:UNIT, :])
                    for _ in range(2):
                        claim("F0")
                        wide("F0", WS[:], ha, K1)
                        claim("F1")
                        wide("F1", WS[:], hb, K1)
                    claim("F0")
                    claim("N0")
                    tall("N0", ha, WS[:, 0:H], H)
                claim("F1")
                if first:
                    claim("N1")
                    tall("N1", hb, WS[:, 0:H], H)
                if second:
                    pe.wait_ge(z2_act, t.take("z2"))
                    pe.wait_ge(z_full["z2"], t.at("z2", 0))
                    claim("F2")
                    transposes("F2", z2[:, 0:HALF, :])
                    transposes("F1", z2[:, HALF:UNIT, :])
                    claim("F2")
                    wide("F2", W1S[:], ga, H)
                    if slots:
                        pe.wait_ge(zg_full, t.take("zg"))
                        transposes("F0", zx[:, 0:HALF, :])
                    claim("F1")
                    wide("F1", W1S[:], gb, H)
                    claim("F2")
                    claim("N0")
                    tall("N0", ga, W2[:], H)
                    if slots:
                        claim("F0")
                        transposes("F0", zx[:, HALF:UNIT, :])
                    claim("F1")
                    claim("N1")
                    tall("N1", gb, W2[:], H)

            nodes(True, False)
            nodes(True, True)
            nodes(True, True)
            per = {"F0": 6, "F1": 10, "F2": 4, "N0": 4, "N1": 4, "z1": 2, "z2": 2}
            with t.loop(pe, SIDES // 2, {**per, "F0": 10, "zg": 2}):
                nodes(True, True, slots=True)
                nodes(True, True, slots=True)
            for q in range(SIDES + 3, LATE):
                nodes(True, True)

            def columns(side, c):
                return lambda lo, n: state[:, bass.ds(side * SLOTS + c * COLS + lo, n)]

            def layer_step(l, turn, u, a, b, f):
                c = 2 * turn + u
                if a and l:
                    pe.wait_ge(g_in[u], 16 * HALF * (EUNITS * (l - 1) + turn + 1))
                    claim("F0")
                    wide("F0", WS[:], columns(0, c), K1, [G[:, u, k, :] for k in range(HALF)])
                if b:
                    pe.wait_ge(scanned, t.take("scan"))
                    claim("N0")
                    tall("N0", S[:, 1 - u], WN[:], K1)
                if f:
                    t_use = t.take("T")
                    if l < 2:
                        pe.wait_ge(t_full, t_use)
                        claim("F1")
                        wide("F1", WS[:], columns(1, c - 2), K1, [T[:, u, k, :] for k in range(HALF)])

            pe.wait_ge(done["F0"], t.at("F0", 0) + 1)
            for l in range(3):
                layer_step(l, 0, 0, True, False, False)
                layer_step(l, 0, 1, True, True, False)
                late = (0, WITH_1, WITH_2)[l]
                layer = {"F0": 2 * (l > 0), "N0": 2, "F1": 2 * (l < 2), "scan": 2, "T": 2}
                if l:
                    both = {name: layer.get(name, 0) + per.get(name, 0) // 2 for name in {**per, **layer}}
                    with t.loop(pe, late, both) as i:
                        for u in range(2):
                            layer_step(l, i + 1, u, True, True, True)
                        nodes(True, True)
                with t.loop(pe, EUNITS - 1 - late, layer) as i:
                    for u in range(2):
                        layer_step(l, i + 1 + late, u, True, True, True)
                layer_step(l, EUNITS, 0, False, True, True)
                layer_step(l, EUNITS, 1, False, False, True)
                for _ in range(1 if l else AFTER_0):
                    nodes(True, True)
            nodes(False, True)

            def last_step(turn, k, a, b, c):
                u, q, use = k % 2, 4 * turn + k, 2 * turn + k // 2
                if a:
                    pe.wait_ge(state_copied, t.take("hc"))
                    pe.wait_ge(g_in[u], 16 * HALF * (2 * EUNITS + use + 1))
                    claim("N0")
                    tall("N0", ha, WS[:, 0:H], H, G[:, u])
                    pe.wait_ge(e_in[u], 16 * 4 * (use + 1))
                    claim("N1")
                    tall("N1", hb, WS[:, 0:H], H, T[:, u])
                if c:
                    pe.wait_ge(h_mixed, t.take("mix"))
                    claim("F1")
                    wide("F1", W1[:], columns(1, q - 2), H)
                if b:
                    pe.wait_ge(z2_act, t.take("z2"))
                    pe.wait_ge(z_full["z2"], t.at("z2", 0))
                    claim("F0")
                    transposes("F0", z2[:, 0:HALF, :])
                    claim("F1")
                    transposes("F1", z2[:, HALF:UNIT, :])
                if c:
                    if not b:
                        claim("F1")
                    claim("N1")
                    tall("N1", gb, W2[:], H)
                if b:
                    claim("F2")
                    pe.wait_ge(done["F0"], t.at("F0"))
                    h = columns(0, q - 1)
                    for lo, n in ((0, 512), (512, COLS - 512)):
                        nc.tensor.matmul(F["F2"][0:H, lo:lo + n], WE[:], ga[:, lo:lo + n], start=True, stop=False)
                        last = nc.tensor.matmul(F["F2"][0:H, lo:lo + n], ident[0:K1, 0:H], h(lo, n),
                                                start=False, stop=True)
                    fill("F2", last)
                if a:
                    claim("F2")
                    transposes("F2", er[:, u])

            for k in range(RING):
                last_step(0, k, True, k > 0, k > 1)
            with t.loop(pe, CHUNKS // RING - 1, {"F0": 4, "F1": 8, "F2": 8, "N0": 4, "N1": 8, "z2": 4, "hc": 4,
                                                 "mix": 4}) as i:
                for k in range(RING):
                    last_step(i + 1, k, True, True, True)
            last_step(CHUNKS // RING, 0, False, True, True)
            last_step(CHUNKS // RING, 1, False, False, True)

        @block.scalar
        def _(act):
            t = Tally()
            for name in F:
                act.sem_inc(done[name], 1)

            def drain(name, to, rows, relu=True, order=False):
                act.wait_ge(full[name], t.take(name))
                if order:
                    act.sem_inc(act_order, 1)
                nc.scalar.activation(to, F[name][0:rows, 0:COLS], ACT.Relu if relu else ACT.Copy)\
                    .then_inc(done[name], 1)

            act.wait_ge(full["F0"], t.take("F0"))
            act.wait_ge(consts_dve, 3)
            for n, (m, w) in enumerate(((WS, 0), (WN, 1), (WE, 2), (W1, 3), (W2, 4))):
                last = nc.scalar.activation(m[0:H, 0:H], F["F0"][0:H, w * H:(w + 1) * H], ACT.Copy)
            last = nc.scalar.activation(W1S[0:H, :], F["F0"][0:H, 3 * H:4 * H], ACT.Copy)
            last.then_inc(done["F0"], 1)

            def normalise(rows, tiles):
                for k in tiles:
                    last = nc.scalar.activation(z2[:, k, 0:H], rows[:, k, :], ACT.Identity,
                                                bias=shift[:, k:k + 1], scale=rstd[:, k:k + 1])
                return last

            def nodes(b, first, second, slots=None):
                for n, tiles in enumerate(ACT_TILES):
                    if first:
                        name, to = (("F0", ha), ("F1", hb))[n % 2]
                        drain(name, to[:], K1)
                    if second and tiles:
                        if not any(ACT_TILES[:n]):
                            act.wait_ge(shift_ready, t.take("shift"))
                        last = normalise(R[:, b], tiles)
                        if not any(ACT_TILES[n + 1:]):
                            last.then_inc(z2_act, 1)
                if second:
                    drain("F2", ga[:], K1)
                    drain("F1", gb[:], K1)
                    drain("F2", ga[0:H, :], H)
                    if slots is not None:
                        drain("F0", state[:, bass.ds(slots * 2 * COLS, COLS)], K1, order=True)
                    drain("F1", gb[0:H, :], H)
                    if slots is not None:
                        drain("F0", state[:, bass.ds(slots * 2 * COLS + COLS, COLS)], K1, order=True)

            nodes(3, True, False)
            nodes(0, True, True)
            nodes(1, True, True)
            per = {"F0": 3 * RING, "F1": 5 * RING, "F2": 2 * RING, "shift": RING}
            with t.loop(act, SIDES // RING, {**per, "F0": 5 * RING}) as i:
                for k in range(RING):
                    nodes((2 + k) % RING, True, True, slots=4 * i + k)
            for q in range(SIDES + 3, LATE):
                nodes((q - 1) % RING, True, True)

            def layer_step(l, c, a, f):
                if a and l:
                    drain("F0", state[:, bass.ds(c * COLS, COLS)], K1, order=True)
                if f and l < 2:
                    drain("F1", state[:, bass.ds(SLOTS + (c - 2) * COLS, COLS)], K1, order=True)

            for l in range(3):
                layer_step(l, 0, True, False)
                layer_step(l, 1, True, False)
                late = (0, WITH_1, WITH_2)[l]
                layer = {"F0": 2 * (l > 0), "F1": 2 * (l < 2)}
                if l == 1:
                    both = {name: RING * layer.get(name, 0) + per[name] for name in per}
                    with t.loop(act, late // RING, both) as i:
                        for k in range(RING):
                            for u in range(2):
                                layer_step(l, 8 * i + (2 + 2 * k + u), True, True)
                            nodes((IN_1 - 1 + k) % RING, True, True)
                if l == 2:
                    for turn in range(1, 1 + late):
                        layer_step(l, 2 * turn, True, True)
                        layer_step(l, 2 * turn + 1, True, True)
                        nodes((IN_2 + turn - 2) % RING, True, True)
                with t.loop(act, EUNITS - 1 - late, layer) as i:
                    for u in range(2):
                        layer_step(l, 2 * i + (2 * late + 2 + u), True, True)
                layer_step(l, CHUNKS, False, True)
                layer_step(l, CHUNKS + 1, False, True)
                for q in (range(LATE, IN_1), [IN_2 - 1], [PAIRS - 1])[l]:
                    nodes((q - 1) % RING, True, True)
            nodes((PAIRS - 1) % RING, False, True)

            act.wait_ge(done["F0"], t.at("F0", 0) + 1)
            act.wait_ge(done["F1"], t.at("F1", 0) + 1)

            def copy_states(q):
                nc.scalar.activation(ha[:], state[:, bass.ds(q * COLS, COLS)], ACT.Copy)
                nc.scalar.activation(hb[:], state[:, bass.ds(SLOTS + q * COLS, COLS)], ACT.Copy)\
                    .then_inc(state_copied, 1)

            def last_step(turn, k, a, b, c, more=True):
                q = 4 * turn + k
                if c:
                    drain("F1", gb[0:H, :], H)
                if b:
                    drain("F0", state[:, bass.ds((q - 1) * COLS, COLS)], K1, order=True)
                    drain("F1", state[:, bass.ds(SLOTS + (q - 1) * COLS, COLS)], K1, order=True)
                if a:
                    act.wait_ge(full["N1"], t.take("N1", 1 + c))
                    act.sem_inc(act_order, 1)
                    if more:
                        copy_states(q + 1)
                if b:
                    drain("F2", state[0:H, bass.ds((q - 1) * COLS, COLS)], H, order=True)
                if a:
                    act.wait_ge(shift_ready, t.take("shift"))
                    normalise(R[:, k], LAST_ACT).then_inc(z2_act, 1)
                    drain("F2", ga[0:H, :], H, relu=False)

            copy_states(0)
            t.base["N1"] = N1_LAST
            for k in range(RING):
                last_step(0, k, True, k > 0, k > 1)
            with t.loop(act, CHUNKS // RING - 2, {"F0": 4, "F1": 8, "F2": 8, "N1": 8, "shift": 4}) as i:
                for k in range(RING):
                    last_step(i + 1, k, True, True, True)
            for k in range(RING):
                last_step(CHUNKS // RING - 1, k, True, True, True, more=k < RING - 1)
            last_step(CHUNKS // RING, 0, False, True, True)
            last_step(CHUNKS // RING, 1, False, False, True)

        @block.vector
        def _(dve):
            t = Tally()
            for name in Nb:
                dve.sem_inc(done[name], 1)
            for u in range(2):
                dve.sem_inc(g_zero[u], 1)
            nc.vector.memset(rows_i[:, 0, :], 0)
            nc.vector.memset(rows_i[:, 1, :], BIG)
            nc.vector.memset(rows_i[:, 2, :], -1)
            nc.vector.memset(big[:], BIG).then_inc(consts_dve, 1)
            nc.vector.memset(S[:], 0.0)
            nc.vector.memset(z1[:], 1.0)
            nc.vector.memset(z2[:], 1.0)
            nc.vector.memset(zx[:], 1.0)
            nc.vector.memset(ga[:], 1.0)
            nc.vector.memset(gb[:], 1.0)
            nc.vector.memset(WS[:], 0.0)
            nc.vector.memset(same[:, 0:1], 0.0)
            nc.vector.memset(WN[:], 0.0).then_inc(consts_dve, 1)

            dve.wait_ge(consts_dve, 2)
            nc.vector.memset(WN[H:K1, H:K1], 1.0)
            nc.vector.memset(WS[H:K1, H:K1], 1.0).then_inc(consts_dve, 1)

            dve.wait_ge(done["F0"], 2)
            dve.wait_ge(loaded_b, 16 * 6)
            nc.vector.tensor_scalar(eps1[:], eps1[:], 1.0, None, ALU.add).then_inc(dve_prep, 1)
            dve.wait_ge(dve_prep, 1)
            nc.vector.tensor_scalar(W1S[0:H, :], W1S[0:H, :], eps1[0:H, :], None, ALU.mult).then_inc(weights_sb, 1)

            dve.wait_ge(loaded_rows, 16 * 6)
            nc.vector.tensor_copy(rows_f[:, 0, :], rows_i[:, 0, :])
            nc.vector.tensor_scalar(rows_f[:, 1, :], rows_i[:, 1, :], float(N_NODES - 1), None, ALU.min)
            nc.vector.tensor_tensor(cont[:], rows_i[:, 1, :], rows_i[:, 2, :], ALU.is_equal).then_inc(dve_prep, 1)
            dve.wait_ge(dve_prep, 2)
            nc.vector.tensor_copy(cont_b[:], cont[:]).then_inc(cont_ready, 1)
            nc.vector.tensor_scalar(cont[:], cont[:], float(BIG), None, ALU.mult).then_inc(dve_prep, 1)
            dve.wait_ge(dve_prep, 3)
            nc.vector.tensor_tensor(rows_f[:, 2, :], cont[:], rows_i[:, 1, :], ALU.add).then_inc(rows_ready, 1)
            dve.wait_ge(full["N0"], t.take("N0"))
            dve.wait_ge(consts_pool, 4)
            idx_t = Nb["N0"]
            nc.vector.tensor_copy(x_idx[:, 0:ETILES], idx_t[:, 0:ETILES]).then_inc(idx_ready, 1)
            nc.vector.tensor_copy(x_idx[:, ETILES:2 * ETILES], idx_t[:, ETILES:2 * ETILES]).then_inc(idx_ready, 1)
            nc.vector.tensor_copy(end_idx[:, :, 0], idx_t[:, 2 * ETILES:3 * ETILES]).then_inc(idx_ready, 1)
            dve.wait_ge(idx_ready, 3)
            dve.sem_inc(done["N0"], 1)

            def tick(last):
                last.then_inc(ln_tick, 1)
                dve.wait_ge(ln_tick, t.take("ln"))

            def statistics(rows, col):
                for k in range(UNIT):
                    last = nc.vector.bn_stats(st[:, col + k, :], rows[:, k, :])
                return last

            def moments(c):
                nc.vector.tensor_tensor(mean[:, c], st[:, c, 1], st[:, c, 4], ALU.add)
                nc.vector.tensor_tensor(diff[:, c], st[:, c, 1], st[:, c, 4], ALU.subtract)
                tick(nc.vector.scalar_tensor_tensor(out=var[:, c], in0=st[:, c, 2], scalar=H * LN_EPS,
                                                    in1=st[:, c, 5], op0=ALU.add, op1=ALU.add))
                nc.vector.tensor_scalar(mean[:, c], mean[:, c], 0.5, None, ALU.mult)
                tick(nc.vector.scalar_tensor_tensor(out=diff[:, c], in0=diff[:, c], scalar=-0.125, in1=diff[:, c],
                                                    op0=ALU.mult, op1=ALU.mult))
                tick(nc.vector.scalar_tensor_tensor(out=var[:, c], in0=var[:, c], scalar=-0.5 / H,
                                                    in1=diff[:, c], op0=ALU.mult, op1=ALU.add))
                tick(nc.vector.tensor_scalar(rstd[:, c].bitcast(i32), var[:, c].bitcast(i32), -0.5, RSQRT_MAGIC,
                                             ALU.mult, ALU.add))
                tick(nc.vector.scalar_tensor_tensor(out=diff[:, c], in0=var[:, c], scalar=3.0 * RSQRT_K,
                                                    in1=rstd[:, c], op0=ALU.mult, op1=ALU.mult))
                tick(nc.vector.tensor_tensor(diff[:, c], diff[:, c], rstd[:, c], ALU.mult))
                tick(nc.vector.scalar_tensor_tensor(out=rstd[:, c], in0=diff[:, c], scalar=1.5 * RSQRT_C,
                                                    in1=rstd[:, c], op0=ALU.add, op1=ALU.mult))
                tick(nc.vector.scalar_tensor_tensor(out=diff[:, c], in0=var[:, c], scalar=1.0 / 2.25,
                                                    in1=rstd[:, c], op0=ALU.mult, op1=ALU.mult))
                tick(nc.vector.tensor_tensor(diff[:, c], diff[:, c], rstd[:, c], ALU.mult))
                tick(nc.vector.scalar_tensor_tensor(out=diff[:, c], in0=diff[:, c], scalar=5.0 / 3.0,
                                                    in1=diff[:, c], op0=ALU.add, op1=ALU.mult))
                tick(nc.vector.scalar_tensor_tensor(out=rstd[:, c], in0=diff[:, c], scalar=1.25,
                                                    in1=rstd[:, c], op0=ALU.add, op1=ALU.mult))

            def normalise(rows, z, col, tiles=range(UNIT)):
                for k in tiles:
                    last = nc.vector.tensor_scalar(z[:, k, 0:H], rows[:, k, :], mean[:, col + k:col + k + 1],
                                                   rstd[:, col + k:col + k + 1], ALU.subtract, ALU.mult)
                return last

            def layernorm(rows, z):
                tick(statistics(rows, UNIT))
                moments(slice(UNIT, 2 * UNIT))
                return normalise(rows, z, UNIT)

            def add_rows(name, to, rows):
                dve.wait_ge(full[name], t.take(name))
                nc.vector.tensor_tensor(to, rows, Nb[name][:, 0:HALF * H].rearrange("p (t f) -> p t f", f=H),
                                        ALU.add).then_inc(done[name], 1)

            lo, hi = slice(0, HALF), slice(HALF, UNIT)

            def nodes(i, k, first=True, second=True, ahead=True, slots=False, slots_before=True,
                      after=True):
                if after:
                    dve.wait_ge(full["F1"], t.at("F1"))
                    normalise(R[:, (k + 3) % RING], z1, UNIT).then_inc(z_full["z1"], 1)
                t.take("F1", 3 * first + 2 * second)
                t.take("F0", 3 * first + 2 * (slots and slots_before))
                mine, before = R[:, (k + 2) % RING], R[:, (k + 1) % RING]
                if first:
                    add_rows("N0", mine[:, lo], mine[:, lo])
                    add_rows("N1", mine[:, hi], mine[:, hi])
                    dve.wait_ge(done["N1"], t.at("N1", 0) + 1)
                    last = statistics(mine, 0)
                    if ahead:
                        dve.wait_ge(x_in[k], 16 * (i + 2))
                        last = statistics(R[:, k], UNIT)
                    if slots:
                        dve.wait_ge(xg_in[k % 2], 16 * UNIT * (2 * i + k // 2 + 1))
                        last = statistics(xg[:, k % 2], 2 * UNIT)
                    tick(last)
                    if second:
                        dve.wait_ge(z2_act, t.take("z2_act"))
                    moments(slice(0, (1 + ahead + slots) * UNIT))
                    nc.vector.scalar_tensor_tensor(out=shift[:], in0=mean[:, 0:UNIT], scalar=-1.0,
                                                   in1=rstd[:, 0:UNIT], op0=ALU.mult, op1=ALU.mult)\
                        .then_inc(shift_ready, 1)
                if second:
                    add_rows("N0", before[:, lo], before[:, lo])
                    add_rows("N1", before[:, hi], before[:, hi])
                if first:
                    if second:
                        dve.wait_ge(full["F1"], t.at("F1", -1))
                    normalise(mine, z2, 0, OWN_TILES).then_inc(z_full["z2"], 1)
                if slots:
                    if slots_before:
                        dve.wait_ge(full["F0"], t.at("F0", 0))
                    normalise(xg[:, k % 2], zx, 2 * UNIT).then_inc(zg_full, 1)

            t.take("F0")
            dve.wait_ge(x_in[0], 16)
            layernorm(R[:, 0], z1).then_inc(z_full["z1"], 1)
            dve.wait_ge(x_in[1], 16)
            tick(statistics(R[:, 1], UNIT))
            moments(slice(UNIT, 2 * UNIT))
            nodes(-1, 2, second=False)
            nodes(-1, 3)
            with_slots = SIDES // RING
            for k in range(RING):
                nodes(0, k, slots=True, slots_before=k > 0)
            per = {"F1": 5 * RING, "F0": 3 * RING, "N0": 2 * RING, "N1": 2 * RING, "ln": RING * LN_TICKS,
                   "z2_act": RING}
            with t.loop(dve, with_slots - 1, {**per, "F0": 5 * RING}) as i:
                for k in range(RING):
                    nodes(i + 1, k, slots=True)
            t.take("F0", 2)
            def step(q, **more):
                nodes((q - 2) // RING, (q - 2) % RING, **more)

            for q in range(SIDES + 2, LATE):
                step(q)

            def scan(c, u, data):
                if not (isinstance(c, int) and c == 0):
                    dve.wait_ge(scanned, t.at("scan", 0))
                nc.vector.tensor_tensor_scan(S[:, u], same[:, bass.ds(c * COLS, COLS)], data,
                                             S[:, 1 - u, COLS - 1:COLS], ALU.mult, ALU.add)\
                    .then_inc(scanned, 1)
                t.take("scan")

            dve.wait_ge(same_ready, 16)
            dve.wait_ge(done["F0"], t.at("F0", 0) + 1)

            def layer_step(l, turn, u, a, b, f, reused=True):
                c = 2 * turn + u
                if a:
                    if l:
                        dve.wait_ge(full["F0"], t.at("F0"))
                        nc.vector.memset(G[:, u], 0.0).then_inc(g_zero[u], 1)
                        dve.wait_ge(done["F0"], t.take("F0") + 1)
                    scan(c, u, state[:, bass.ds(c * COLS, COLS)])
                if b:
                    dve.wait_ge(full["N0"], t.take("N0"))
                    sums = Nb["N0"][:, 0:HALF * K1].rearrange("p (t f) -> p t f", f=K1)
                    degrees = rdeg[:, bass.ds((c - 1) * HALF, HALF)]
                    if l == 0:
                        nc.vector.reciprocal(degrees, sums[:, :, H]).then_inc(deg_done, 1)
                        dve.wait_ge(deg_done, t.take("deg"))
                    if reused:
                        dve.wait_ge(t_out[1 - u], 16 * (l * EUNITS + turn - 1 + u))
                        dve.wait_ge(full["F1"], t.at("F1", 0))
                    nc.vector.tensor_tensor(T[:, 1 - u], sums[:, :, 0:H],
                                            degrees.unsqueeze(2).broadcast_to([P, HALF, H]),
                                            ALU.mult).then_inc(t_full, 1)
                    dve.wait_ge(t_full, t.take("T"))
                    dve.sem_inc(done["N0"], 1)
                if f:
                    t.take("F1", int(l < 2))

            for l in range(3):
                layer_step(l, 0, 0, True, False, False)
                layer_step(l, 0, 1, True, True, False, reused=l > 0)
                start = 1
                if l == 0:
                    layer_step(l, 1, 0, True, True, True, reused=False)
                    layer_step(l, 1, 1, True, True, True)
                    start = 2
                layer = {"scan": 2, "N0": 2, "T": 2, "deg": 2 * (l == 0), "F1": 2 * (l < 2), "F0": 2 * (l > 0)}
                if l == 1:
                    with t.loop(dve, WITH_1 // RING, {name: RING * layer.get(name, 0) + per.get(name, 0)
                                                    for name in {**per, **layer}}) as i:
                        for k in range(RING):
                            for u in range(2):
                                layer_step(l, 4 * i + (1 + k), u, True, True, True)
                            nodes(i + (IN_1 - 2 + k) // RING, (IN_1 - 2 + k) % RING)
                    start += WITH_1
                if l == 2:
                    for turn in range(1, 1 + WITH_2):
                        for u in range(2):
                            layer_step(l, turn, u, True, True, True)
                        q = IN_2 + turn - 1
                        step(q, ahead=q < PAIRS - 2)
                    start += WITH_2
                with t.loop(dve, EUNITS - start, layer) as i:
                    for u in range(2):
                        layer_step(l, i + start, u, True, True, True)
                layer_step(l, EUNITS, 0, False, True, True)
                layer_step(l, EUNITS, 1, False, False, True)
                for q in (range(LATE, IN_1), [IN_2 - 1], [PAIRS - 1])[l]:
                    step(q, ahead=l < 2, after=l < 2)
            step(PAIRS, first=False, ahead=False, after=False)
            t.take("F2", F2_LAST)


            def last_step(turn, k, a, b, c, reused=True):
                u, q, use = k % 2, 4 * turn + k, 2 * turn + k // 2
                if a:
                    dve.wait_ge(e_in[u], 16 * 4 * (use + 1))
                    if reused:
                        dve.wait_ge(yo[u], 16 * HALF * (use - 1))
                    else:
                        dve.wait_ge(y_out[k], 16 * (PAIRS // RING))
                    add_rows("N0", R[:, k, lo], xg[:, u, lo])
                    add_rows("N1", R[:, k, hi], xg[:, u, hi])
                    nc.vector.memset(G[:, u], 0.0).then_inc(g_zero[u], 1)
                    dve.wait_ge(done["N1"], t.at("N1", 0) + 1)
                    tick(statistics(R[:, k], 0))
                    dve.wait_ge(z2_act, t.take("z2_act"))
                    moments(slice(0, UNIT))
                    nc.vector.scalar_tensor_tensor(out=shift[:], in0=mean[:, 0:UNIT], scalar=-1.0,
                                                   in1=rstd[:, 0:UNIT], op0=ALU.mult, op1=ALU.mult)\
                        .then_inc(shift_ready, 1)
                if c:
                    t.take("F1")
                    r = R[:, (k - 2) % RING, hi]
                    add_rows("N1", r, r)
                if b:
                    dve.wait_ge(done["F2"], t.take("F2") + 1)
                    dve.wait_ge(scanned, t.at("scan", 0))
                    nc.vector.tensor_tensor_scan(S[0:H, 1 - u], same[0:H, bass.ds((q - 1) * COLS, COLS)],
                                                 state[0:H, bass.ds((q - 1) * COLS, COLS)],
                                                 S[0:H, u, COLS - 1:COLS],
                                                 ALU.mult, ALU.add).then_inc(scanned, 1)
                    dve.wait_ge(scanned, t.take("scan"))
                    dve.wait_ge(done["F1"], t.take("F1") + 1)
                    h = state[0:H, bass.ds(SLOTS + (q - 1) * COLS, COLS)]
                    nc.vector.scalar_tensor_tensor(out=h, in0=h, scalar=eps1[0:H, :], in1=S[0:H, 1 - u],
                                                   op0=ALU.mult, op1=ALU.add).then_inc(h_mixed, 1)
                if a:
                    t.take("F2")
                    own = [k for k in range(UNIT) if k not in LAST_ACT]
                    normalise(R[:, k], z2, 0, own).then_inc(z_full["z2"], 1)

            for k in range(RING):
                last_step(0, k, True, k > 0, k > 1, reused=False)
            with t.loop(dve, CHUNKS // RING - 1, {"N0": 4, "N1": 8, "ln": 4 * LN_TICKS, "F2": 8, "F1": 8,
                                                  "scan": 4, "z2_act": 4}) as i:
                for k in range(RING):
                    last_step(i + 1, k, True, True, True)
            last_step(CHUNKS // RING, 0, False, True, True)
            last_step(CHUNKS // RING, 1, False, False, True)


_INS = ["x", "src", "dst", "edge_attr_96", "L0_gnn_W_self", "L0_gnn_W_neigh", "L0_gnn_b", "L1_gnn_W_edge",
        "L1_gnn_b_edge", "L1_gnn_eps", "L1_gnn_W1", "L1_gnn_b1", "L1_gnn_W2", "L1_gnn_b2"]


def kernel(**inputs):
    import concourse.bacc as bacc
    from concourse.bass_utils import run_bass_kernel_spmd

    nc = bacc.Bacc("TRN2", target_bir_lowering=False, num_devices=1)
    arrays, args = {}, []
    for name in _INS:
        a = np.ascontiguousarray(inputs[name])
        if a.ndim == 0:
            a = a.reshape(1)
        arrays["in_" + name] = a
        args.append(nc.dram_tensor("in_" + name, a.shape, mybir.dt.from_np(a.dtype), kind="ExternalInput").ap())
    out = nc.dram_tensor("out", (N_NODES, H), f32, kind="ExternalOutput").ap()
    (x, src, dst, edge_attr, w_self, w_neigh, b, w_edge, b_edge, eps, w1, b1, w2, b2) = args
    build(nc, x, src, dst, edge_attr, w_self, w_neigh, b, w_edge, b_edge, eps, w1, b1, w2, b2, out)
    return run_bass_kernel_spmd(nc, [arrays], core_ids=[0]).results[0]["out"]
```
